# Optimizing a Trainium2 kernel written in Bass

```python
import numpy as np
import jax
import jax.numpy as jnp

def _softmax(x, axis=-1):
    return jax.nn.softmax(x, axis=axis)

def _gelu(x):
    return jax.nn.gelu(x, approximate=True)

def _silu(x):
    return jax.nn.silu(x)

def _sigmoid(x):
    return jax.nn.sigmoid(x)

def _layernorm(x, axis=-1, eps=1e-05):
    m = jnp.mean(x, axis=axis, keepdims=True)
    v = jnp.var(x, axis=axis, keepdims=True)
    return (x - m) / jnp.sqrt(v + eps)

def _scatter_add(tgt, idx, src, axis=0):
    return tgt.at[idx].add(src)

def _segment_sum(src, seg, n):
    return jax.ops.segment_sum(src, seg, n)
kernel_name = 'mk_macaron_d1_jaxref_r8_83222c'

def setup_inputs(seed: int=0):
    np.random.seed(seed)
    _w = jnp.asarray

    def _L0_attn_setup():
        import jax, jax.numpy as jnp
        import numpy as np
        import math
        NUM_HEADS = 16

        def get_slopes(n):

            def pow2(n):
                start = 2 ** (-2 ** (-(math.log2(n) - 3)))
                return [start * start ** i for i in range(n)]
            if math.log2(n).is_integer():
                return pow2(n)
            c = 2 ** math.floor(math.log2(n))
            return pow2(c) + get_slopes(2 * c)[0::2][:n - c]
        key = jax.random.key(seed)
        ks = jax.random.split(key, 5)
        B, T, C = (2, 256, 128)
        return {'x': jax.random.normal(ks[0], (B, T, C), dtype=jnp.float32), 'W_qkv': jax.random.normal(ks[1], (C, 3 * C), dtype=jnp.float32) * 0.02, 'b_qkv': jax.random.normal(ks[2], (3 * C,), dtype=jnp.float32) * 0.02, 'W_proj': jax.random.normal(ks[3], (C, C), dtype=jnp.float32) * 0.02, 'b_proj': jax.random.normal(ks[4], (C,), dtype=jnp.float32) * 0.02}
    _L0_attn_in = _L0_attn_setup()

    def _L0_ffn_setup():
        import jax, jax.numpy as jnp
        import numpy as np
        B, S, D = (2, 256, 128)
        I = 64
        E = 16
        TOP_K = 2

        def _mlp(x, wg, wu, wd):
            return jnp.einsum('bsi,id->bsd', jax.nn.silu(x @ wg) * (x @ wu), wd)
        key = jax.random.key(seed)
        ks = jax.random.split(key, 10)
        sc_d = 1.0 / np.sqrt(D)
        sc_i = 1.0 / np.sqrt(I)
        return {'x': jax.random.normal(ks[0], (B, S, D), dtype=jnp.float32), 'gate_w': jax.random.normal(ks[1], (D, E), dtype=jnp.float32) * sc_d, 'gate_b': jnp.zeros((E,), dtype=jnp.float32), 'shared_wg': jax.random.normal(ks[2], (D, I), dtype=jnp.float32) * sc_d, 'shared_wu': jax.random.normal(ks[3], (D, I), dtype=jnp.float32) * sc_d, 'shared_wd': jax.random.normal(ks[4], (I, D), dtype=jnp.float32) * sc_i, 'experts_wg': jax.random.normal(ks[5], (E, D, I), dtype=jnp.float32) * sc_d, 'experts_wu': jax.random.normal(ks[6], (E, D, I), dtype=jnp.float32) * sc_d, 'experts_wd': jax.random.normal(ks[7], (E, I, D), dtype=jnp.float32) * sc_i}
    _L0_ffn_in = _L0_ffn_setup()
    _d = {'L0_attn_x': _L0_attn_in['x'], 'L0_attn_W_qkv': _L0_attn_in['W_qkv'], 'L0_attn_b_qkv': _L0_attn_in['b_qkv'], 'L0_attn_W_proj': _L0_attn_in['W_proj'], 'L0_attn_b_proj': _L0_attn_in['b_proj'], 'L0_ffn_gate_w': _L0_ffn_in['gate_w'], 'L0_ffn_gate_b': _L0_ffn_in['gate_b'], 'L0_ffn_shared_wg': _L0_ffn_in['shared_wg'], 'L0_ffn_shared_wu': _L0_ffn_in['shared_wu'], 'L0_ffn_shared_wd': _L0_ffn_in['shared_wd'], 'L0_ffn_experts_wg': _L0_ffn_in['experts_wg'], 'L0_ffn_experts_wu': _L0_ffn_in['experts_wu'], 'L0_ffn_experts_wd': _L0_ffn_in['experts_wd']}
    _x0 = _d['L0_attn_x']
    _d['L0_attn_x'] = jax.random.normal(jax.random.fold_in(jax.random.key(seed), 1), (2, 1024, 128), dtype=_x0.dtype)
    del _x0
    return _d

def reference(L0_attn_x, L0_attn_W_qkv, L0_attn_b_qkv, L0_attn_W_proj, L0_attn_b_proj, L0_ffn_gate_w, L0_ffn_gate_b, L0_ffn_shared_wg, L0_ffn_shared_wu, L0_ffn_shared_wd, L0_ffn_experts_wg, L0_ffn_experts_wu, L0_ffn_experts_wd):

    def _L0_attn_ref(x, W_qkv, b_qkv, W_proj, b_proj):
        import jax, jax.numpy as jnp
        import numpy as np
        import math
        NUM_HEADS = 16

        def get_slopes(n):

            def pow2(n):
                start = 2 ** (-2 ** (-(math.log2(n) - 3)))
                return [start * start ** i for i in range(n)]
            if math.log2(n).is_integer():
                return pow2(n)
            c = 2 ** math.floor(math.log2(n))
            return pow2(c) + get_slopes(2 * c)[0::2][:n - c]
        B, T, C = x.shape
        H = NUM_HEADS
        D = C // H
        qkv = x @ W_qkv + b_qkv
        q, k, v = jnp.split(qkv, 3, axis=-1)
        q = q.reshape(B, T, H, D).transpose(0, 2, 1, 3)
        k = k.reshape(B, T, H, D).transpose(0, 2, 1, 3)
        v = v.reshape(B, T, H, D).transpose(0, 2, 1, 3)
        slopes = jnp.asarray(get_slopes(H), dtype=jnp.float32)
        idx = jnp.arange(T)
        alibi = jnp.minimum(idx[None, :] - idx[:, None], 0).astype(jnp.float32)
        bias = slopes[:, None, None] * alibi
        scale = 1.0 / math.sqrt(D)
        scores = jnp.einsum('bhtd,bhsd->bhts', q, k) * scale + bias[None]
        w = jax.nn.softmax(scores, axis=-1)
        y = jnp.einsum('bhts,bhsd->bhtd', w, v)
        y = y.transpose(0, 2, 1, 3).reshape(B, T, C)
        return y @ W_proj + b_proj

    def _L0_ffn_ref(x, gate_w, gate_b, shared_wg, shared_wu, shared_wd, experts_wg, experts_wu, experts_wd):
        import jax, jax.numpy as jnp
        import numpy as np
        B, S, D = (2, 256, 128)
        I = 64
        E = 16
        TOP_K = 2

        def _mlp(x, wg, wu, wd):
            return jnp.einsum('bsi,id->bsd', jax.nn.silu(x @ wg) * (x @ wu), wd)
        router_logits = jax.nn.sigmoid(x @ gate_w + gate_b)
        expert_values, expert_indices = jax.lax.top_k(router_logits, k=TOP_K)
        expert_values = expert_values / jnp.sum(expert_values, axis=-1, keepdims=True)
        hg = jnp.einsum('bsd,edi->bsei', x, experts_wg)
        hu = jnp.einsum('bsd,edi->bsei', x, experts_wu)
        all_outputs = jnp.einsum('bsei,eid->bsed', jax.nn.silu(hg) * hu, experts_wd)
        selected = jnp.take_along_axis(all_outputs, expert_indices[..., None], axis=2)
        expert_weighted = jnp.sum(expert_values[..., None] * selected, axis=2)
        return x + _mlp(x, shared_wg, shared_wu, shared_wd) + expert_weighted
    x = L0_attn_x
    x = x + 0.5 * _L0_ffn_ref(_layernorm(x, axis=-1), L0_ffn_gate_w, L0_ffn_gate_b, L0_ffn_shared_wg, L0_ffn_shared_wu, L0_ffn_shared_wd, L0_ffn_experts_wg, L0_ffn_experts_wu, L0_ffn_experts_wd)
    x = x + _L0_attn_ref(_layernorm(x, axis=-1), L0_attn_W_qkv, L0_attn_b_qkv, L0_attn_W_proj, L0_attn_b_proj)
    x = x + 0.5 * _L0_ffn_ref(_layernorm(x, axis=-1), L0_ffn_gate_w, L0_ffn_gate_b, L0_ffn_shared_wg, L0_ffn_shared_wu, L0_ffn_shared_wd, L0_ffn_experts_wg, L0_ffn_experts_wu, L0_ffn_experts_wd)
    return x

_drawn_inputs = setup_inputs


def setup_inputs(seed=0):
    import zlib

    import numpy as np

    out = dict(_drawn_inputs(seed))
    spreads = {'L0_ffn_gate_b': (0.0, 0.1)}
    factors = {'L0_attn_W_qkv': 8.0, 'L0_attn_b_qkv': 8.0, 'L0_attn_W_proj': 8.0, 'L0_attn_b_proj': 3.217}
    for name, (base, spread) in spreads.items():
        noise = np.random.default_rng([zlib.crc32(name.encode()), seed]).standard_normal(out[name].shape)
        drawn = base * np.exp(spread * noise) if base else spread * noise
        out[name] = jnp.asarray(drawn.astype(out[name].dtype))
    for name, factor in factors.items():
        out[name] = (out[name] * factor).astype(out[name].dtype)
    return out
```

```python
from contextlib import ExitStack

import concourse.bass as bass
import numpy as np
from concourse import mybir

F32 = mybir.dt.float32
BF16 = mybir.dt.bfloat16
ALU = mybir.AluOpType
ACT = mybir.ActivationFunctionType
AX_X = mybir.AxisListType.X

P = 128
B, T, C = 2, 1024, 128
H = 16
DH = C // H
NT = B * T // P
TB = T // P
E = 16
I = 64
NCH = E // 2
SLAB = 512
NS = B * T // SLAB
TPS = SLAB // P
EPS = 1e-5
GH = 4
NG = B * H // GH
SPLIT = ((0, 0), (0, 1), (1, 0), (0, 2), (2, 0), (1, 1))
ROWS_D = len(SPLIT) * DH
ROWS_B = 2 * 3 * TB
ROWS_1 = ROWS_D + ROWS_B
ROWS_2 = ROWS_1 + 3
SCALE = float(DH) ** -0.5
VW = 32


def slopes():
    start = 2.0 ** (-(2.0 ** -(np.log2(H) - 3)))
    return np.array([start * start ** i for i in range(H)], np.float32)


def bf16_parts(a):
    parts, rest = [], np.asarray(a, np.float64)
    for _ in range(3):
        p = rest.astype(mybir.dt.np(BF16))
        parts.append(p)
        rest = rest - p.astype(np.float64)
    return parts


def constants():
    bf = mybir.dt.np(BF16)
    sl = slopes().astype(np.float64)
    pos = np.arange(T)
    blk = pos // P
    j = np.arange(TB)
    coef = (blk[None, :] > j[:, None]) + 0.5 * (blk[None, :] == j[:, None])
    away = pos[None, :] - P * j[:, None]
    here = (blk[None, :] == j[:, None]).astype(np.float64)
    q = np.zeros((ROWS_B, H, T), bf)
    for h in range(H):
        for p, part in enumerate(bf16_parts(sl[h] * coef)):
            q[p * TB:(p + 1) * TB, h] = part
        for p, part in enumerate(bf16_parts(-sl[h] * coef * away)):
            q[(3 + p) * TB:(4 + p) * TB, h] = part
    k = np.ones((ROWS_B + 3, T), bf)
    k[0:3 * TB] = np.tile(away * here, (3, 1)).astype(bf)
    k[3 * TB:6 * TB] = np.tile(here, (3, 1)).astype(bf)
    d = np.abs(np.arange(P)[:, None] - np.arange(P)[None, :])
    table = (-0.5 * sl[None, :, None] * d[:, None, :])
    table = table[:, np.arange((NG + 1) * GH) % H]
    sel = np.zeros((3, E, NCH, 2, I), bf)
    for e in range(E):
        sel[:, e, e // 2, e % 2, :] = 0.25
    return {
        "identity": np.eye(P, dtype=np.float32),
        "identity_bf": np.eye(P).astype(bf),
        "select": sel.reshape(3 * E, NCH * P),
        "q_bias": q.reshape(ROWS_B, H * T),
        "k_bias": k,
        "decay": table.reshape(P, -1).astype(np.float32),
        "decay_exp": np.exp(table).reshape(P, -1).astype(np.float32),
    }


class Mem:
    pass


def allocate(nc, ctx):
    m = Mem()

    def sb(name, cols, dt=F32, rows=P):
        return ctx.enter_context(nc.sbuf_tensor(name, [rows, cols], dt))

    m.x = sb("x", NT * C)[:, :].rearrange("p (n c) -> p n c", n=NT)
    m.q = sb("q_rows", NG * GH * T, BF16)
    m.k = sb("k_rows", NG * GH * T, BF16)
    m.pool = sb("pool", 12288)
    m.v = sb("v_all", NG * TB * GH * DH)
    m.y = sb("y_group", T)
    m.vcur = sb("v_group", TB * GH * VW)
    m.ident = sb("identity_s", P)
    m.ident_bf = sb("identity_bf_s", P, BF16)
    m.gate_w = sb("gate_w_s", E)
    m.gate_b = sb("gate_b_s", E)
    m.w_proj = sb("w_proj_s", C)
    m.b_proj = sb("b_proj_s", C)
    m.b_qk = sb("b_qk_s", 2)
    m.stats = sb("stats", NT * 6)
    m.mv = sb("mean_var", NT * 2)
    m.rs = sb("rstd", NT * 4)
    m.max_a = sb("max_off_diagonal", GH * TB)
    m.max_b = sb("max_diagonal", GH * TB)
    m.max_parts = sb("max_parts", 3 * GH * TB, BF16)
    m.max_rows = sb("max_rows", P, BF16)
    m.junk = sb("junk", 2 * P)
    m.recip = sb("recip", TB * GH)
    m.bias_loaded = ctx.enter_context(nc.semaphore("bias_loaded"))
    m.rows_loaded = [ctx.enter_context(nc.semaphore(f"rows_loaded{b}")) for b in range(B)]
    m.decay_loaded = ctx.enter_context(nc.semaphore("decay_loaded"))
    m.proj_loaded = ctx.enter_context(nc.semaphore("proj_loaded"))
    m.ps = ctx.enter_context(nc.psum_tensor("psum", [P, 8 * 512], F32))
    return m


def layer_norm(m, x_n, xT, sems):
    link_sem, var_ready, sd_ready, xn_ready, xt_psum, xt_ready = sems
    st = m.stats[:, :].rearrange("p (n c) -> p n c", n=NT)
    mv = m.mv[:, :].rearrange("p (n c) -> p n c", n=NT)
    rs = m.rs[:, :].rearrange("p (k n) -> p k n", k=4)
    var_eps, sd, r, t = rs[:, 0], rs[:, 1], rs[:, 2], rs[:, 3]

    def on_vector(dve, link):
        for n in range(NT):
            last = dve.bn_stats(st[:, n], m.x[:, n])
        link(last)
        for n in range(NT):
            last = dve.bn_aggr(mv[:, n], st[:, n])
        link(last)
        dve.tensor_scalar(var_eps, mv[:, :, 1], EPS, None, ALU.add).then_inc(var_ready, 1)
        dve.wait_ge(sd_ready, 1)
        link(dve.reciprocal(r, sd))
        link(dve.tensor_tensor(t, r, r, ALU.mult))
        link(dve.tensor_tensor(sd, t, var_eps, ALU.mult))
        link(dve.tensor_scalar(t, sd, -0.5, 1.5, ALU.mult, ALU.add))
        link(dve.tensor_tensor(sd, t, r, ALU.mult))
        for n in range(NT):
            dve.tensor_scalar(x_n[:, n], m.x[:, n], mv[:, n, 0:1], sd[:, n:n + 1],
                              ALU.subtract, ALU.mult).then_inc(xn_ready, 1)

    def on_scalar(act):
        act.wait_ge(var_ready, 1)
        act.activation(sd, var_eps, ACT.Sqrt).then_inc(sd_ready, 1)
        for s in range(NS):
            act.wait_ge(xt_psum, s + 1)
            act.activation(xT[:, s * SLAB:(s + 1) * SLAB], m.ps[:, s * 512:(s + 1) * 512],
                           ACT.Copy).then_inc(xt_ready, 1)

    def on_tensor(pe):
        for s in range(NS):
            for j in range(TPS):
                n = s * TPS + j
                pe.wait_ge(xn_ready, n + 1)
                last = pe.transpose(m.ps[:, n * P:(n + 1) * P], x_n[:, n], m.ident[:, :])
            last.then_inc(xt_psum, 1)

    return on_vector, on_scalar, on_tensor


class Chain:

    def __init__(self, eng, sem):
        self.eng, self.sem, self.done = eng, sem, 0

    def __call__(self, ins):
        self.done += 1
        ins.then_inc(self.sem, 1)
        self.eng.wait_ge(self.sem, self.done)


def ffn_phase(nc, m, name, d, x_in, x_out):
    with ExitStack() as ctx:
        def sem(what):
            return ctx.enter_context(nc.semaphore(f"{name}_{what}"))

        pool = m.pool[:, :]
        cut = [0]

        def take(cols):
            cut[0] += cols
            return pool[:, cut[0] - cols:cut[0]]

        w_gate = take(E * I).rearrange("p (c k) -> p c k", c=NCH)
        w_up = take(E * I).rearrange("p (c k) -> p c k", c=NCH)
        w_sh = take(2 * I)
        w_down = take((NCH + 1) * C).rearrange("p (c k) -> p c k", c=NCH + 1)
        select = take(NCH * P // 2).bitcast(BF16)
        x_n = take(NT * C).rearrange("p (n c) -> p n c", n=NT)
        xT = take(NT * P)
        wT = take(NT * P // 2).bitcast(BF16)
        sig = take(NT * 24).rearrange("p (n e) -> p n e", n=NT)
        rep = take(NT * 24).rearrange("p (n e) -> p n e", n=NT)
        top = take(NT * 8).rearrange("p (n e) -> p n e", n=NT)
        two = take(NT * 8).rearrange("p (n e) -> p n e", n=NT)
        sums = take(NT)
        inv = take(NT)
        wts = take(NT * E).rearrange("p (n e) -> p n e", n=NT)
        parts = take(NT * 3 * E // 2).bitcast(BF16).rearrange("p (n k e) -> p n k e", n=NT, k=3)
        th = [m.v[:, s * SLAB:(s + 1) * SLAB] for s in range(3)]
        hid = [m.y[:, 0:SLAB], m.y[:, SLAB:2 * SLAB], m.v[:, 3 * SLAB:4 * SLAB]]
        silu, gated = m.vcur[:, 0:SLAB], m.vcur[:, SLAB:2 * SLAB]

        ps = m.ps
        bank = [ps[:, b * 512:(b + 1) * 512] for b in range(8)]
        gate_ps, up_ps, wt_ps = bank[0:2], bank[2:4], bank[4:6]
        shared_ps, out_ps = bank[6], bank[7]
        logit_ps = bank[7][:, 0:NT * E].rearrange("p (n e) -> p n e", n=NT)
        wT_ps = ps[0:3 * E, 4 * 512:6 * 512].bitcast(BF16)

        x_in_s, const_s, route_s, weights_s = sem("x_in"), sem("const"), sem("route"), sem("weights")
        link_s = sem("link")
        ln = [link_s, sem("var"), sem("sd"), sem("xn"), sem("xt_psum"), sem("xt")]
        xt_ready = ln[5]
        logits_s, z_s, tanh_s = sem("logits"), sem("z"), sem("tanh")
        parts_s, wt_psum_s, wt_s = sem("parts"), sem("wt_psum"), sem("wt")
        gu_s = sem("gate_up")
        th_s = sem("tanh_gate")
        hid_s = sem("hidden")
        down_s = sem("down")
        x_s = sem("x_new")
        store_s = sem("store")
        ln_vector, ln_scalar, ln_tensor = layer_norm(m, x_n, xT, ln)
        last = NS - 1

        with nc.Block() as block:

            @block.sync
            def _(sp):
                if x_in is not None:
                    for s in range(2):
                        sp.dma_start(m.x[:, s * NT // 2:(s + 1) * NT // 2],
                                     x_in[:, s * NT // 2:(s + 1) * NT // 2]).then_inc(x_in_s, 16)
                    sp.dma_start(m.ident[:, :], d["identity"]).then_inc(const_s, 16)
                    sp.dma_start(m.ident_bf[:, :], d["identity_bf"]).then_inc(const_s, 16)
                    sp.dma_start(m.gate_w[:, :], d["gate_w"]).then_inc(route_s, 16)
                    sp.dma_start(m.gate_b[:, :], d["gate_b"].partition_broadcast(P)).then_inc(route_s, 16)
                sp.dma_start(select[0:3 * E], d["select"]).then_inc(weights_s, 16)
                sp.dma_start(w_gate.rearrange("p c (e i) -> p (c e) i", e=2),
                             d["experts_wg"].rearrange("e d i -> d e i")).then_inc(weights_s, 16)
                sp.dma_start(w_up.rearrange("p c (e i) -> p (c e) i", e=2),
                             d["experts_wu"].rearrange("e d i -> d e i")).then_inc(weights_s, 16)
                sp.dma_start(w_sh[:, 0:I], d["shared_wg"]).then_inc(weights_s, 16)
                sp.dma_start(w_sh[:, I:2 * I], d["shared_wu"]).then_inc(weights_s, 16)
                sp.dma_start(w_down[:, 0:NCH], d["experts_wd"].rearrange("(c e) i d -> (e i) c d", e=2)
                             ).then_inc(weights_s, 16)
                sp.dma_start(w_down[0:I, NCH], d["shared_wd"]).then_inc(weights_s, 16)
                if x_in is not None:
                    for b in range(B):
                        sp.dma_start(m.q[ROWS_D:ROWS_1, b * H * T:(b + 1) * H * T], d["q_bias"]
                                     ).then_inc(m.bias_loaded, 16)
                        sp.dma_start(m.k[ROWS_D:ROWS_2, b * H * T:(b + 1) * H * T].rearrange(
                            "p (h t) -> p h t", h=H), d["k_bias"].unsqueeze(1).to_broadcast([ROWS_B + 3, H, T])
                                     ).then_inc(m.bias_loaded, 16)
                if x_out is not None:
                    for s in range(NS):
                        sp.wait_ge(x_s, s + 1)
                        sp.dma_start(x_out[:, s * TPS:(s + 1) * TPS],
                                     m.x[:, s * TPS:(s + 1) * TPS]).then_inc(store_s, 16)
                    sp.wait_ge(store_s, 16 * NS)

            @block.scalar
            def _(act):
                ln_scalar(act)
                act.wait_ge(z_s, 1)
                act.activation(wts, wts, ACT.Tanh, scale=0.5).then_inc(tanh_s, 1)
                for s in range(2):
                    act.wait_ge(wt_psum_s, s + 1)
                    act.activation(wT[0:3 * E, s * 1024:(s + 1) * 1024],
                                   wT_ps[:, s * 1024:(s + 1) * 1024], ACT.Copy).then_inc(wt_s, 1)
                def slab(s):
                    for c in range(NCH + 1):
                        act.wait_ge(gu_s, s * (NCH + 1) + c + 1)
                        rows = slice(0, P) if c < NCH else slice(0, I)
                        gate = gate_ps[c % 2] if c < NCH else shared_ps[rows]
                        act.activation(th[c % 3][rows], gate, ACT.Tanh, scale=0.5).then_inc(th_s, 1)

                with act.Fori(0, NS) as s:
                    slab(s)

            @block.vector
            def _(dve):
                link = Chain(dve, link_s)
                if x_in is not None:
                    dve.wait_ge(x_in_s, 32)
                ln_vector(dve, link)
                dve.memset(sig, -1.0)
                link(dve.memset(two, -1.0))
                link(dve.scalar_tensor_tensor(m.x, x_n, 0.5, m.x, ALU.mult, ALU.add))
                if x_in is not None:
                    dve.wait_ge(route_s, 32)
                dve.wait_ge(logits_s, 1)
                dve.tensor_tensor(wts, logit_ps, m.gate_b[:, :].unsqueeze(1).to_broadcast([P, NT, E]),
                                  ALU.add).then_inc(z_s, 1)
                dve.wait_ge(tanh_s, 1)
                link(dve.tensor_scalar(sig[:, :, 0:E], wts, 0.5, 0.5, ALU.mult, ALU.add))
                for n in range(NT):
                    ins = dve.max(top[:, n], sig[:, n, 0:E])
                link(ins)
                link(dve.tensor_copy(two[:, :, 0:2], top[:, :, 0:2]))
                for n in range(NT):
                    ins = dve.match_replace(rep[:, n], two[:, n], sig[:, n], 0.0)
                link(ins)
                dve.tensor_tensor(wts, sig[:, :, 0:E], rep[:, :, 0:E], ALU.subtract)
                link(dve.tensor_tensor(sums, top[:, :, 0], top[:, :, 1], ALU.add))
                link(dve.reciprocal(inv, sums))
                link(dve.tensor_tensor(wts, wts, inv.unsqueeze(2).to_broadcast([P, NT, E]), ALU.mult))
                link(dve.tensor_copy(parts[:, :, 0], wts))
                link(dve.tensor_tensor(wts, wts, parts[:, :, 0], ALU.subtract))
                link(dve.tensor_copy(parts[:, :, 1], wts))
                dve.tensor_tensor(parts[:, :, 2], wts, parts[:, :, 1], ALU.subtract).then_inc(parts_s, 1)

                base = link.done

                def slab(s):
                    for c in range(NCH + 1):
                        n = s * (NCH + 1) + c
                        k = base + s * (2 * NCH + 1) + 2 * c
                        dve.wait_ge(th_s, n + 1)
                        shared = c == NCH
                        rows = slice(0, I) if shared else slice(0, P)
                        gate = shared_ps[rows] if shared else gate_ps[c % 2]
                        dve.scalar_tensor_tensor(silu[rows], th[c % 3][rows], 1.0, gate,
                                                 ALU.add, ALU.mult).then_inc(link_s, 1)
                        dve.wait_ge(link_s, k + 1)
                        if c >= 3:
                            dve.wait_ge(down_s, n - 2)
                        if shared:
                            dve.scalar_tensor_tensor(hid[c % 3][rows], silu[rows], 0.25, shared_ps[I:2 * I],
                                                     ALU.mult, ALU.mult).then_inc(hid_s, 1)
                            continue
                        dve.tensor_tensor(gated, silu, up_ps[c % 2], ALU.mult).then_inc(link_s, 1)
                        dve.wait_ge(link_s, k + 2)
                        dve.tensor_tensor(hid[c % 3], gated, wt_ps[c % 2], ALU.mult).then_inc(hid_s, 1)
                    dve.wait_ge(down_s, (s + 1) * (NCH + 1))
                    xs = m.x[:, bass.ts(s, TPS)]
                    dve.tensor_tensor(xs, out_ps.rearrange("p (n c) -> p n c", n=TPS), xs,
                                      ALU.add).then_inc(x_s, 1)

                with dve.Fori(0, NS) as s:
                    slab(s)

            @block.tensor
            def _(pe):
                if x_in is not None:
                    pe.wait_ge(const_s, 32)
                ln_tensor(pe)
                if x_in is not None:
                    pe.wait_ge(route_s, 32)
                for n in range(NT):
                    if n % TPS == 0:
                        pe.wait_ge(xt_ready, n // TPS + 1)
                    ins = pe.matmul(logit_ps[:, n], xT[:, n * P:(n + 1) * P], m.gate_w[:, :],
                                    start=True, stop=True)
                ins.then_inc(logits_s, 1)
                pe.wait_ge(parts_s, 1)
                for n in range(NT):
                    ins = pe.transpose(wT_ps[:, n * P:(n + 1) * P],
                                       parts[:, n].rearrange("p k e -> p (k e)"), m.ident_bf[:, :])
                    if n % (NT // 2) == NT // 2 - 1:
                        ins.then_inc(wt_psum_s, 1)

                def products(s, c):
                    moving = xT[:, bass.ts(s, SLAB)]
                    if c == NCH:
                        pe.matmul(shared_ps, w_sh, moving, start=True, stop=True).then_inc(gu_s, 1)
                        return
                    pe.matmul(gate_ps[c % 2], w_gate[:, c], moving, start=True, stop=True)
                    pe.matmul(up_ps[c % 2], w_up[:, c], moving, start=True, stop=True)
                    pe.matmul(wt_ps[c % 2], select[0:3 * E, c * P:(c + 1) * P],
                              wT[0:3 * E, bass.ts(s, SLAB)], start=True, stop=True).then_inc(gu_s, 1)

                def down(s, c):
                    pe.wait_ge(hid_s, s * (NCH + 1) + c + 1)
                    rows = slice(0, P) if c < NCH else slice(0, I)
                    for j in range(TPS):
                        ins = pe.matmul(out_ps[:, j * P:(j + 1) * P], hid[c % 3][rows, j * P:(j + 1) * P],
                                        w_down[rows, c], start=(c == 0 and j == 0), stop=(c == NCH),
                                        skip_group_check=True)
                    ins.then_inc(down_s, 1)

                def slab(s, more):
                    for c in range(NCH + 1):
                        nxt = c + 2
                        if nxt <= NCH:
                            if nxt < NCH:
                                pe.wait_ge(hid_s, s * (NCH + 1) + nxt - 1)
                            products(s, nxt)
                        elif more:
                            pe.wait_ge(hid_s, s * (NCH + 1) + NCH - 1 + nxt - NCH - 1)
                            products(s + 1, nxt - NCH - 1)
                        down(s, c)
                    if more:
                        pe.wait_ge(x_s, s + 1)

                pe.wait_ge(weights_s, 16 * 7)
                pe.wait_ge(wt_s, 2)
                for c in range(2):
                    products(0, c)
                with pe.Fori(0, NS - 1) as s:
                    slab(s, True)
                slab(NS - 1, False)


def qkv_phase(nc, m, d, scratch):
    with ExitStack() as ctx:
        def sem(what):
            return ctx.enter_context(nc.semaphore(f"qkv_{what}"))

        x_n = m.pool[:, 0:2048].rearrange("p (n c) -> p n c", n=NT)
        xT = m.pool[:, 2048:4096]
        parts = m.pool[:, 4096:10240].bitcast(BF16).rearrange("p (b w k t) -> p b w k t", b=B, w=2, k=3)
        decay = m.pool[:, 10240:10240 + GH * P]
        w_qkv = m.vcur[:, 0:3 * C]
        b_v = m.vcur[:, 3 * C:4 * C]
        rest = [m.y[:, 0:SLAB], m.y[:, SLAB:2 * SLAB]]
        v = m.v[:, :].rearrange("p (b g t k) -> p b g t k", b=B, g=H // GH, t=TB)
        bank = [m.ps[:, b * 512:(b + 1) * 512] for b in range(8)]
        qk_ps = bank[4:8] + bank[0:4]
        v_ps = bank[4:8]

        link_s = sem("link")
        ln = [link_s, sem("var"), sem("sd"), sem("xn"), sem("xt_psum"), sem("xt")]
        xt_ready = ln[5]
        w_s, qk_s, v_s = sem("weights"), sem("qk_psum"), sem("v_psum")
        full_s = sem("full")
        p1_s, r1_s, p2_s, p3_s = sem("part1"), sem("rest1"), sem("part2"), sem("part3")
        vdone_s = sem("v_sbuf")
        stored = [sem(f"stored{b}") for b in range(B)]
        ln_vector, ln_scalar, ln_tensor = layer_norm(m, x_n, xT, ln)
        order = [(s, w) for s in range(NS) for w in range(2)]

        def part(s, w, k):
            b, at = s * SLAB // T, s * SLAB % T
            return parts[:, b, w, k, at:at + SLAB]

        with nc.Block() as block:

            @block.sync
            def _(sp):
                sp.dma_start(w_qkv, d["W_qkv"]).then_inc(w_s, 16)
                sp.dma_start(b_v, d["b_qkv"][2 * C:3 * C].partition_broadcast(P)).then_inc(w_s, 16)
                for w in range(2):
                    sp.dma_start(m.b_qk[:, w:w + 1], d["b_qkv"][w * C:(w + 1) * C].unsqueeze(1)).then_inc(w_s, 16)
                sp.dma_start(decay, d["decay"][:, 0:GH * P]).then_inc(m.decay_loaded, 16)
                for b in range(B):
                    sp.wait_ge(p3_s, (b + 1) * len(order) // B)
                    for w in range(2):
                        for k in range(3):
                            sp.dma_start(scratch[b, w, k], parts[:, b, w, k]).then_inc(stored[b], 16)
                    sp.wait_ge(stored[b], 16 * 6)
                    for w, rows in enumerate((m.q, m.k)):
                        for slot, which in enumerate(SPLIT):
                            sp.dma_start(
                                rows[slot * DH:(slot + 1) * DH, b * H * T:(b + 1) * H * T].rearrange(
                                    "p (h t) -> p h t", h=H),
                                scratch[b, w, which[w]].rearrange("(h e) t -> e h t", e=DH)
                            ).then_inc(m.rows_loaded[b], 16)
                sp.dma_start(m.w_proj[:, :], d["W_proj"]).then_inc(m.proj_loaded, 16)
                sp.dma_start(m.b_proj[:, :], d["b_proj"].partition_broadcast(P)).then_inc(m.proj_loaded, 16)

            @block.scalar
            def _(act):
                ln_scalar(act)
                for n, (s, w) in enumerate(order):
                    act.wait_ge(full_s, n + 1)
                    act.activation(part(s, w, 0), rest[n % 2], ACT.Copy).then_inc(p1_s, 1)
                    act.wait_ge(r1_s, n + 1)
                    act.activation(part(s, w, 1), rest[n % 2], ACT.Copy).then_inc(p2_s, 1)

            @block.gpsimd
            def _(pool):
                for n, (s, w) in enumerate(order):
                    pool.wait_ge(p2_s, n + 1)
                    pool.tensor_tensor(part(s, w, 2), rest[n % 2], part(s, w, 1), ALU.subtract).then_inc(p3_s, 1)

            @block.vector
            def _(dve):
                link = Chain(dve, link_s)
                ln_vector(dve, link)
                dve.wait_ge(w_s, 64)

                def full(n):
                    s, w = order[n]
                    dve.wait_ge(qk_s, n + 1)
                    if n >= 2:
                        dve.wait_ge(p3_s, n - 1)
                    dve.tensor_scalar(rest[n % 2], qk_ps[n], m.b_qk[:, w:w + 1], SCALE if w == 0 else 1.0,
                                      ALU.add, ALU.mult).then_inc(full_s, 1)

                full(0)
                for n, (s, w) in enumerate(order):
                    if n + 1 < len(order):
                        full(n + 1)
                    dve.wait_ge(p1_s, n + 1)
                    dve.tensor_tensor(rest[n % 2], rest[n % 2], part(s, w, 0), ALU.subtract).then_inc(r1_s, 1)
                for n in range(NT):
                    b, t = divmod(n, TB)
                    if n % TPS == 0:
                        dve.wait_ge(v_s, n // TPS + 1)
                    dve.tensor_tensor(v[:, b, :, t], v_ps[n // TPS][:, n % TPS * P:(n % TPS + 1) * P].rearrange(
                        "p (g k) -> p g k", g=H // GH), b_v.rearrange("p (g k) -> p g k", g=H // GH),
                        ALU.add).then_inc(vdone_s, 1)

            @block.tensor
            def _(pe):
                ln_tensor(pe)
                pe.wait_ge(xt_ready, NS)
                pe.wait_ge(w_s, 64)
                for n, (s, w) in enumerate(order):
                    pe.matmul(qk_ps[n], w_qkv[:, w * C:(w + 1) * C], xT[:, s * SLAB:(s + 1) * SLAB],
                              start=True, stop=True).then_inc(qk_s, 1)
                for n in range(NT):
                    if n % TPS == 0:
                        pe.wait_ge(full_s, n // TPS + 1)
                    ins = pe.matmul(v_ps[n // TPS][:, n % TPS * P:(n % TPS + 1) * P], xT[:, n * P:(n + 1) * P],
                                    w_qkv[:, 2 * C:3 * C], start=True, stop=True)
                    if n % TPS == TPS - 1:
                        ins.then_inc(v_s, 1)


QUADS = 2 * TB
UNITS = QUADS * GH
TILES = GH * TB
TILES_IN = [3, 3, 3, 3] + [2] * 10 + [0, 0]
TURN = 3
USES = TILES + 2
RESULTS_AT = sum(TILES_IN[:TURN])
LAG = 2
SLOTS = 4


def attention_phase(nc, m, d):
    with ExitStack() as ctx:
        def sem(what):
            return ctx.enter_context(nc.semaphore(f"att_{what}"))

        probs = m.pool[:, 0:SLOTS * GH * SLAB].rearrange("p (s j t) -> p s j t", s=SLOTS, j=GH)
        decay = m.pool[:, 10240:10240 + GH * P]
        decay_exp = m.pool[:, 8192:8192 + GH * P]
        v_group = m.vcur[:, :].rearrange("p (t j k) -> p t j k", t=TB, j=GH)
        double = [m.ps[:, 0:1024], m.ps[:, 1024:2048]]
        score_ps = [m.ps[:, 2048:2560], m.ps[:, 2560:3072]]
        acc_ps = m.ps[:, 3072:4096]
        parts = m.max_parts[:, :].rearrange("p (k n) -> p k n", k=3)
        recip = m.recip[:, :].rearrange("p (t j) -> p t j", t=TB)

        vinit_s = sem("v_init")
        exp_table_s = sem("decay_exp")
        table_s = sem("decay")
        d_ready_s = sem("double_ready")
        d_free_s = sem("double_free")
        link_s = sem("link")
        parts_s = sem("max_parts")
        rows_s = sem("max_rows")
        score_s = sem("scores")
        exp_s = sem("exp")
        decay_s = sem("decayed")
        pv_s = sem("pv")
        y_s = sem("y")
        vg_s = sem("v_group")

        def early(g):
            return isinstance(g, int) and g < 2

        def start_of(g):
            return g * USES - (g if early(g) else 2)

        def tile_use(g, t):
            return t if t < RESULTS_AT or early(g) else t + 1

        def maxima_use(g):
            return USES - 2 if early(g) else USES - 1

        def turn_of(g, n):
            return (start_of(g) + n if early(g) else n) % 2

        def has_diagonal(q):
            return q // 2 // (TB // 2) == q % 2

        def group_cols(g, start, size):
            return bass.ds(g * (GH * T) + start, size)

        with nc.Block() as block:

            @block.sync
            def _(sp):
                def rows(g):
                    sp.wait_ge(d_free_s, start_of(g) + maxima_use(g) + 1)
                    for k in range(3):
                        sp.dma_start(m.q[ROWS_1 + k:ROWS_1 + k + 1, group_cols(g, 0, GH * T)].rearrange(
                            "o (n t) -> o n t", n=TILES), m.max_rows[k * TILES:(k + 1) * TILES, :]
                        ).then_inc(rows_s, 16)

                def table_of(name, g):
                    return d[name][:, bass.ds(g * (GH * P), GH * P)]

                def body(g, first, last):
                    if not first:
                        sp.wait_ge(decay_s, g * TB)
                    sp.dma_start(decay_exp, table_of("decay_exp", g)).then_inc(exp_table_s, 16)
                    if last:
                        return
                    sp.wait_ge(d_free_s, start_of(g + 1) + maxima_use(g + 1))
                    sp.dma_start(decay, table_of("decay", g + 2)).then_inc(table_s, 16)
                    rows(g + 1)

                sp.wait_ge(d_free_s, maxima_use(0))
                sp.dma_start(decay, table_of("decay", 1)).then_inc(table_s, 16)
                rows(0)
                body(0, True, False)
                with sp.Fori(1, NG - 1) as g:
                    body(g, False, False)
                body(NG - 1, False, True)
                sp.wait_ge(table_s, NG * 16)

            @block.gpsimd
            def _(pool):
                pool.memset(m.vcur[:, :], 0.0).then_inc(vinit_s, 1)
                pool.wait_ge(vinit_s, 1)
                pool.memset(v_group[:, :, :, DH:DH + 1], 1.0).then_inc(vinit_s, 1)
                pool.wait_ge(vinit_s, 2)

                def body(g, first):
                    n = 0
                    pool.wait_ge(exp_table_s, 16 * (g + 1))
                    for q in range(QUADS):
                        if q == 1:
                            if not first:
                                pool.wait_ge(pv_s, g * QUADS)
                            pool.tensor_copy(v_group[:, :, :, 0:DH], m.v[:, bass.ts(g, TB * GH * DH)].rearrange(
                                "p (t j k) -> p t j k", t=TB, j=GH)).then_inc(vg_s, 1)
                        if not has_diagonal(q):
                            continue
                        pool.wait_ge(exp_s, g * UNITS + (q + 1) * GH)
                        at = q // 2 % (TB // 2) * P
                        block_ = probs[:, q % SLOTS, :, at:at + P]
                        pool.tensor_tensor(block_, block_, decay_exp.rearrange("p (j t) -> p j t", j=GH),
                                           ALU.mult).then_inc(decay_s, 1)
                        n += 1
                    assert n == TB

                body(0, True)
                with pool.Fori(1, NG) as g:
                    body(g, False)

            @block.scalar
            def _(act):
                def result(g):
                    act.wait_ge(pv_s, (g + 1) * QUADS)
                    for n in range(2):
                        act.activation(m.y[:, n * SLAB:(n + 1) * SLAB], acc_ps[:, n * SLAB:(n + 1) * SLAB],
                                       ACT.Copy).then_inc(y_s, 1)

                def body(g, first):
                    for q in range(QUADS):
                        if not first or q >= SLOTS:
                            act.wait_ge(pv_s, g * QUADS + q - SLOTS + 1)
                        for j in range(GH):
                            u = q * GH + j
                            act.wait_ge(score_s, g * UNITS + u + 1)
                            act.activation(probs[:, q % SLOTS, j], score_ps[u % 2], ACT.Exp).then_inc(exp_s, 1)
                        if q == LAG - 1 and not first:
                            result(g - 1)

                body(0, True)
                with act.Fori(1, NG) as g:
                    body(g, False)
                result(NG - 1)

            @block.vector
            def _(dve):
                link = Chain(dve, link_s)
                dve.wait_ge(m.decay_loaded, 16)

                def tile(g, t):
                    n = tile_use(g, t)
                    u = start_of(g) + n
                    dve.wait_ge(d_ready_s, u + 1)
                    ps = double[turn_of(g, n)]
                    j = t // TB
                    if t == 0 and not (isinstance(g, int) and g == 0):
                        dve.wait_ge(table_s, 16 * g)
                    if not isinstance(u, int) or u > 1:
                        dve.wait_ge(d_free_s, u - 1)
                    dve.tensor_reduce(m.max_a[:, t:t + 1], ps[:, 0:T - P], AX_X, ALU.max)
                    dve.tensor_tensor_reduce(
                        m.junk[:, turn_of(g, n) * P:(turn_of(g, n) + 1) * P], ps[:, T - P:T],
                        decay[:, j * P:(j + 1) * P], 1.0, -3.0e38, ALU.add, ALU.max,
                        m.max_b[:, t:t + 1]).then_inc(d_free_s, 1)

                def split(g):
                    u = start_of(g) + maxima_use(g)
                    k = split_links(g)
                    dve.wait_ge(d_free_s, u)
                    dve.tensor_tensor(m.max_a[:, :], m.max_a[:, :], m.max_b[:, :], ALU.max).then_inc(link_s, 1)
                    dve.wait_ge(link_s, k + 1)
                    dve.tensor_scalar(parts[:, 0], m.max_a[:, :], -1.0, None, ALU.mult).then_inc(link_s, 1)
                    dve.wait_ge(link_s, k + 2)
                    dve.scalar_tensor_tensor(m.max_b[:, :], m.max_a[:, :], -1.0, parts[:, 0],
                                             ALU.mult, ALU.subtract).then_inc(link_s, 1)
                    dve.wait_ge(link_s, k + 3)
                    dve.tensor_copy(parts[:, 1], m.max_b[:, :]).then_inc(link_s, 1)
                    dve.wait_ge(link_s, k + 4)
                    dve.tensor_tensor(parts[:, 2], m.max_b[:, :], parts[:, 1], ALU.subtract).then_inc(parts_s, 1)
                    dve.wait_ge(d_ready_s, u + 1)
                    if not isinstance(g, int) or g > 0:
                        dve.wait_ge(rows_s, g * 48)
                    dve.tensor_copy(m.max_rows[0:3 * TILES, :], double[turn_of(g, maxima_use(g))][
                        0:3 * TILES, 0:P // 2].bitcast(BF16)).then_inc(d_free_s, 1)

                def split_links(g):
                    return 4 * g if early(g) else 5 * g - 1

                def result(g, u, turn, links):
                    dve.wait_ge(d_ready_s, u + 1)
                    ps = double[turn].rearrange("p (t j k) -> p t j k", t=TB, j=GH)
                    dve.reciprocal(recip, ps[:, :, :, DH]).then_inc(link_s, 1)
                    dve.wait_ge(link_s, links + 1)
                    dve.tensor_tensor(m.v[:, bass.ts(g, TB * GH * DH)].rearrange("p (t j k) -> p t j k", t=TB, j=GH),
                                      ps[:, :, :, 0:DH], recip.unsqueeze(3).to_broadcast([P, TB, GH, DH]),
                                      ALU.mult).then_inc(d_free_s, 1)

                def body(g, first, last):
                    t = 0
                    for q in range(QUADS):
                        if q == TURN and last:
                            result(g - 1, start_of(NG), turn_of(NG, 0), split_links(NG) - 1)
                        elif q == TURN and not first:
                            result(g - 1, start_of(g + 1) + RESULTS_AT, turn_of(g + 1, RESULTS_AT),
                                   split_links(g + 1) - 1)
                        if last:
                            continue
                        for _ in range(TILES_IN[q]):
                            tile(g + 1, t)
                            t += 1
                    if not last:
                        split(g + 1)

                for t in range(TILES):
                    tile(0, t)
                split(0)
                body(0, True, False)
                with dve.Fori(1, NG - 1) as g:
                    body(g, False, False)
                body(NG - 1, False, True)
                dve.wait_ge(d_free_s, start_of(NG) + 1)
                result(NG - 1, start_of(NG) + 1, turn_of(NG, 1), split_links(NG))

            @block.tensor
            def _(pe):
                def double_free(g, n):
                    u = start_of(g) + n
                    if not isinstance(u, int) or u > 1:
                        pe.wait_ge(d_free_s, u - 1)

                def tile(g, t):
                    n = tile_use(g, t)
                    double_free(g, n)
                    j, i = divmod(t, TB)
                    order = [s for s in range(TB) if s != i] + [i]
                    at = 0
                    while at < TB:
                        size = 1
                        while (at + size) % (TB // 2) and order[at + size:] and order[at + size] == order[at] + size:
                            size += 1
                        ins = pe.matmul(double[turn_of(g, n)][:, at * P:(at + size) * P],
                                        m.q[0:ROWS_1, group_cols(g, j * T + i * P, P)],
                                        m.k[0:ROWS_1, group_cols(g, j * T + order[at] * P, size * P)],
                                        start=True, stop=True)
                        at += size
                    ins.then_inc(d_ready_s, 1)

                def maxima(g):
                    double_free(g, maxima_use(g))
                    pe.wait_ge(parts_s, g + 1)
                    pe.transpose(double[turn_of(g, maxima_use(g))][0:3 * TILES, 0:P // 2].bitcast(BF16),
                                 m.max_parts[:, :], m.ident_bf[:, :]).then_inc(d_ready_s, 1)

                def result(g, u_group, n):
                    double_free(u_group, n)
                    pe.wait_ge(y_s, 2 * (g + 1))
                    for t in range(TB):
                        ins = pe.transpose(double[turn_of(u_group, n)][:, t * P:(t + 1) * P], m.y[:, t * P:(t + 1) * P],
                                           m.ident[:, :])
                    ins.then_inc(d_ready_s, 1)

                def scores(g, q, j):
                    u = q * GH + j
                    s, n = divmod(q, 2)
                    if not isinstance(g, int) or g > 0 or u >= 2:
                        pe.wait_ge(exp_s, g * UNITS + u - 1)
                    pe.matmul(score_ps[u % 2], m.k[0:ROWS_2, group_cols(g, j * T + s * P, P)],
                              m.q[0:ROWS_2, group_cols(g, j * T + n * SLAB, SLAB)],
                              start=True, stop=True).then_inc(score_s, 1)

                def pv(g, q):
                    s, n = divmod(q, 2)
                    if has_diagonal(q):
                        pe.wait_ge(decay_s, g * TB + sum(has_diagonal(x) for x in range(q + 1)))
                    else:
                        pe.wait_ge(exp_s, g * UNITS + (q + 1) * GH)
                    if q == 0:
                        pe.wait_ge(vg_s, g + 1)
                        if not isinstance(g, int) or g > 0:
                            pe.wait_ge(y_s, 2 * g)
                    for j in range(GH):
                        ins = pe.matmul(acc_ps[32 * j:32 * (j + 1), n * SLAB:(n + 1) * SLAB], v_group[:, s, j],
                                        probs[:, q % SLOTS, j], start=(s == 0), stop=(s == TB - 1),
                                        skip_group_check=True)
                    ins.then_inc(pv_s, 1)

                def body(g, first, last):
                    t = 0
                    for q in range(QUADS):
                        if q == 0:
                            pe.wait_ge(rows_s, 48 * (g + 1))
                        if q == TURN and not first:
                            if last:
                                result(g - 1, NG, 0)
                            else:
                                result(g - 1, g + 1, RESULTS_AT)
                        todo = 0 if last else TILES_IN[q]
                        for j in range(GH):
                            scores(g, q, j)
                            if j % 2 == 1 or j == 0 and todo == 3:
                                if t < TILES and todo > 0 and not last:
                                    tile(g + 1, t)
                                    t += 1
                                    todo -= 1
                        if q >= LAG:
                            pv(g, q - LAG)
                        elif not first:
                            pv(g - 1, QUADS - LAG + q)
                        if q == QUADS - 2 and not last:
                            maxima(g + 1)

                pe.wait_ge(m.bias_loaded, 16 * 2 * B)
                for b in range(B):
                    pe.wait_ge(m.rows_loaded[b], 16 * 2 * len(SPLIT))
                for t in range(TILES):
                    tile(0, t)
                maxima(0)
                body(0, True, False)
                with pe.Fori(1, NG - 1) as g:
                    body(g, False, False)
                body(NG - 1, False, True)
                for q in range(QUADS - LAG, QUADS):
                    pv(NG - 1, q)
                result(NG - 1, NG, 1)


def project_phase(nc, m):
    with ExitStack() as ctx:
        def sem(what):
            return ctx.enter_context(nc.semaphore(f"proj_{what}"))

        yT = m.pool[:, 0:NT * P]
        y = m.pool[:, NT * P:2 * NT * P].rearrange("p (b t g k) -> p b t g k", b=B, g=H // GH, t=TB)
        v = m.v[:, :].rearrange("p (b g t k) -> p b g t k", b=B, g=H // GH, t=TB)
        y_s, turned_s, yt_s, out_s, bias_s, x_s = sem("y"), sem("turned"), sem("yT"), sem("out"), sem("bias"), sem("x")

        with nc.Block() as block:

            @block.scalar
            def _(act):
                for s in range(NS):
                    act.wait_ge(turned_s, s + 1)
                    act.activation(yT[:, s * SLAB:(s + 1) * SLAB], m.ps[:, s * 512:(s + 1) * 512],
                                   ACT.Copy).then_inc(yt_s, 1)

            @block.vector
            def _(dve):
                for b in range(B):
                    dve.tensor_copy(y[:, b].rearrange("p t g k -> p g t k"), v[:, b]).then_inc(y_s, 1)
                dve.wait_ge(m.proj_loaded, 32)
                dve.tensor_tensor(m.x, m.x, m.b_proj[:, :].unsqueeze(1).to_broadcast([P, NT, C]),
                                  ALU.add).then_inc(bias_s, 1)
                dve.wait_ge(bias_s, 1)
                for s in range(NS):
                    dve.wait_ge(out_s, s + 1)
                    xs = m.x[:, s * TPS:(s + 1) * TPS]
                    dve.tensor_tensor(xs, m.ps[:, (4 + s) * 512:(5 + s) * 512].rearrange("p (n c) -> p n c", n=TPS),
                                      xs, ALU.add).then_inc(x_s, 1)
                dve.wait_ge(x_s, NS)

            @block.tensor
            def _(pe):
                for n in range(NT):
                    b, t = divmod(n, TB)
                    if t == 0:
                        pe.wait_ge(y_s, b + 1)
                    ins = pe.transpose(m.ps[:, n * P:(n + 1) * P], y[:, b, t].rearrange("p g k -> p (g k)"),
                                       m.ident[:, :])
                    if n % TPS == TPS - 1:
                        ins.then_inc(turned_s, 1)
                pe.wait_ge(m.proj_loaded, 32)
                for n in range(NT):
                    if n % TPS == 0:
                        pe.wait_ge(yt_s, n // TPS + 1)
                    ins = pe.matmul(m.ps[:, 2048 + n * P:2048 + (n + 1) * P], yT[:, n * P:(n + 1) * P],
                                    m.w_proj[:, :], start=True, stop=True)
                    if n % TPS == TPS - 1:
                        ins.then_inc(out_s, 1)


def build(nc, d, x_in, out, scratch):
    with ExitStack() as ctx:
        m = allocate(nc, ctx)
        ffn_phase(nc, m, "ffn1", d, x_in, None)
        qkv_phase(nc, m, d, scratch)
        attention_phase(nc, m, d)
        project_phase(nc, m)
        ffn_phase(nc, m, "ffn2", d, None, out)


_INS = ["L0_attn_x", "L0_attn_W_qkv", "L0_attn_b_qkv", "L0_attn_W_proj", "L0_attn_b_proj", "L0_ffn_gate_w",
        "L0_ffn_gate_b", "L0_ffn_shared_wg", "L0_ffn_shared_wu", "L0_ffn_shared_wd", "L0_ffn_experts_wg",
        "L0_ffn_experts_wu", "L0_ffn_experts_wd"]


def kernel(**inputs):
    import concourse.bacc as bacc
    from concourse.bass_utils import run_bass_kernel_spmd

    nc = bacc.Bacc("TRN2", target_bir_lowering=False, num_devices=1)
    arrays, d = {}, {}
    given = {k: np.ascontiguousarray(inputs[k]) for k in _INS}
    for name, a in {**given, **constants()}.items():
        key = f"in_{name}_dram"
        arrays[key] = a
        short = name.replace("L0_ffn_", "").replace("L0_attn_", "")
        d[short] = nc.dram_tensor(key, a.shape, mybir.dt.from_np(a.dtype), kind="ExternalInput").ap()
    out = nc.dram_tensor("out_0_dram", (B, T, C), F32, kind="ExternalOutput").ap()
    tiled = "b (t p) c -> p (b t) c"
    scratch = nc.dram_tensor("parts_dram", (B, 2, 3, C, T), BF16, kind="Internal").ap()
    build(nc, d, d["x"].rearrange(tiled, p=P), out.rearrange(tiled, p=P), scratch)
    r = run_bass_kernel_spmd(nc, [arrays], core_ids=[0])
    return r.results[0]["out_0_dram"]
```

```python
from contextlib import ExitStack

import concourse.bass as bass
import numpy as np
from concourse import mybir

F32 = mybir.dt.float32
F32R = mybir.dt.float32r
BF16 = mybir.dt.bfloat16
ALU = mybir.AluOpType
ACT = mybir.ActivationFunctionType
AX_X = mybir.AxisListType.X

P = 128
B, T, C = 2, 1024, 128
H = 16
DH = C // H
NT = B * T // P
TB = T // P
E = 16
I = 64
NCH = E // 2
SLAB = 512
NS = B * T // SLAB
TPS = SLAB // P
EPS = 1e-5
GH = 4
NG = B * H // GH
SPLIT = ((0, 0), (0, 1), (0, 2), (1, 0), (1, 1), (2, 0))
RUNS = ((0, 3), (3, 5), (5, 6))
ROWS_D = len(SPLIT) * DH
ROWS_B = 2 * 3 * TB
ROWS_1 = ROWS_D + ROWS_B
ROWS_2 = ROWS_1 + 3
SCALE = float(DH) ** -0.5
VW = 32


def slopes():
    start = 2.0 ** (-(2.0 ** -(np.log2(H) - 3)))
    return np.array([start * start ** i for i in range(H)], np.float32)


def bf16_parts(a):
    parts, rest = [], np.asarray(a, np.float64)
    for _ in range(3):
        p = rest.astype(mybir.dt.np(BF16))
        parts.append(p)
        rest = rest - p.astype(np.float64)
    return parts


def constants():
    bf = mybir.dt.np(BF16)
    sl = slopes().astype(np.float64)
    pos = np.arange(T)
    blk = pos // P
    j = np.arange(TB)
    coef = (blk[None, :] > j[:, None]) + 0.5 * (blk[None, :] == j[:, None])
    away = pos[None, :] - P * j[:, None]
    here = (blk[None, :] == j[:, None]).astype(np.float64)
    q = np.zeros((ROWS_B, H, T), bf)
    for h in range(H):
        for p, part in enumerate(bf16_parts(sl[h] * coef)):
            q[p * TB:(p + 1) * TB, h] = part
        for p, part in enumerate(bf16_parts(-sl[h] * coef * away)):
            q[(3 + p) * TB:(4 + p) * TB, h] = part
    k = np.ones((ROWS_B + 3, T), bf)
    k[0:3 * TB] = np.tile(away * here, (3, 1)).astype(bf)
    k[3 * TB:6 * TB] = np.tile(here, (3, 1)).astype(bf)
    k[ROWS_B:] = -1
    d = np.abs(np.arange(P)[:, None] - np.arange(P)[None, :])
    table = (-0.5 * sl[None, :, None] * d[:, None, :])
    table = table[:, np.arange(NG * GH) % H]
    sel = np.zeros((3, E, NCH, 2, I), bf)
    for e in range(E):
        sel[:, e, e // 2, e % 2, :] = 0.25
    return {
        "identity": np.eye(P, dtype=np.float32),
        "identity_bf": np.eye(P).astype(bf),
        "select": sel.reshape(3 * E, NCH * P),
        "q_bias": np.ascontiguousarray(q.reshape(ROWS_B, H // GH, GH, 2, T // 2).swapaxes(2, 3)
                                       ).reshape(ROWS_B, H * T),
        "k_bias": k,
        "decay": table.reshape(P, -1).astype(np.float32),
        "decay_exp": np.exp(table).reshape(P, -1).astype(np.float32),
    }


class Mem:
    pass


def allocate(nc, ctx):
    m = Mem()

    def sb(name, cols, dt=F32, rows=P):
        return ctx.enter_context(nc.sbuf_tensor(name, [rows, cols], dt))

    m.x = sb("x", NT * C)[:, :].rearrange("p (n c) -> p n c", n=NT)
    m.q = sb("q_rows", H * T, BF16)
    m.k = sb("k_rows", H * T, BF16)
    m.w_gu = [sb(f"w_gate_up_{k}", (2 * NCH + 1) * P, F32R) for k in ("high", "low")]
    m.w_dn = [sb(f"w_down_{k}", (NCH + 1) * C, F32R) for k in ("high", "low")]
    m.w_gate = [sb(f"w_route_{k}", E, F32R) for k in ("high", "low")]
    m.select = sb("select_s", NCH * P, BF16)
    m.v = sb("v_all", NG * TB * GH * DH)
    m.y = sb("y_group", T)
    m.vcur = sb("v_group", TB * GH * VW)
    m.ident = sb("identity_s", P)
    m.ident_bf = sb("identity_bf_s", P, BF16)
    m.gate_b = sb("gate_b_s", E)
    m.w_proj = sb("w_proj_s", C)
    m.b_proj = sb("b_proj_s", C)
    m.b_qk = sb("b_qk_s", 2)
    m.stats = sb("stats", NT * 6)
    m.mv = sb("mean_var", NT * 2)
    m.rs = sb("rstd", NT * 4)
    m.max_a = sb("max_off_diagonal", GH * TB)
    m.max_b = sb("max_diagonal", GH * TB)
    m.max_parts = sb("max_parts", 3 * GH * TB, BF16)
    m.max_rows = sb("max_rows", P, BF16)
    m.decay = [sb(f"decay_{h}", GH * P) for h in range(2)]
    m.junk = sb("junk", 2 * P)
    m.recip = sb("recip", TB * GH)
    m.bias_loaded = ctx.enter_context(nc.semaphore("bias_loaded"))
    m.rows_0 = ctx.enter_context(nc.semaphore("rows_of_group_0"))
    m.rows = ctx.enter_context(nc.semaphore("rows_of_later_groups"))
    m.decay_loaded = [ctx.enter_context(nc.semaphore(f"decay_loaded_{h}")) for h in range(2)]
    m.proj_loaded = ctx.enter_context(nc.semaphore("proj_loaded"))
    m.ps = ctx.enter_context(nc.psum_tensor("psum", [P, 8 * 512], F32))
    return m


def layer_norm(m, x_n, xT, xT_low, sems):
    link_sem, var_ready, sd_ready, xn_ready, xt_psum, xt_ready, low_ready = sems
    st = m.stats[:, :].rearrange("p (n c) -> p n c", n=NT)
    mv = m.mv[:, :].rearrange("p (n c) -> p n c", n=NT)
    rs = m.rs[:, :].rearrange("p (k n) -> p k n", k=4)
    var_eps, sd, r, t = rs[:, 0], rs[:, 1], rs[:, 2], rs[:, 3]

    def on_vector(dve, link):
        for n in range(NT):
            last = dve.bn_stats(st[:, n], m.x[:, n])
        link(last)
        for n in range(NT):
            last = dve.bn_aggr(mv[:, n], st[:, n])
        link(last)
        dve.tensor_scalar(var_eps, mv[:, :, 1], EPS, None, ALU.add).then_inc(var_ready, 1)
        dve.wait_ge(sd_ready, 1)
        link(dve.reciprocal(r, sd))
        link(dve.tensor_tensor(t, r, r, ALU.mult))
        link(dve.tensor_tensor(sd, t, var_eps, ALU.mult))
        link(dve.tensor_scalar(t, sd, -0.5, 1.5, ALU.mult, ALU.add))
        link(dve.tensor_tensor(sd, t, r, ALU.mult))
        for n in range(NT):
            dve.tensor_scalar(x_n[:, n], m.x[:, n], mv[:, n, 0:1], sd[:, n:n + 1],
                              ALU.subtract, ALU.mult).then_inc(xn_ready, 1)

    def low_on_vector(dve):
        for s in range(NS):
            cols = slice(s * SLAB, (s + 1) * SLAB)
            dve.wait_ge(xt_ready, s + 1)
            dve.tensor_tensor(xT_low[:, cols], m.ps[:, s * 512:(s + 1) * 512], xT[:, cols].bitcast(F32),
                              ALU.subtract).then_inc(low_ready, 1)

    def on_scalar(act):
        act.wait_ge(var_ready, 1)
        act.activation(sd, var_eps, ACT.Sqrt).then_inc(sd_ready, 1)
        for s in range(NS):
            act.wait_ge(xt_psum, s + 1)
            act.activation(xT[:, s * SLAB:(s + 1) * SLAB], m.ps[:, s * 512:(s + 1) * 512],
                           ACT.Copy).then_inc(xt_ready, 1)

    def on_tensor(pe):
        for s in range(NS):
            for j in range(TPS):
                n = s * TPS + j
                pe.wait_ge(xn_ready, n + 1)
                last = pe.transpose(m.ps[:, n * P:(n + 1) * P], x_n[:, n], m.ident[:, :])
            last.then_inc(xt_psum, 1)

    return on_vector, low_on_vector, on_scalar, on_tensor


class Chain:

    def __init__(self, eng, sem):
        self.eng, self.sem, self.done = eng, sem, 0

    def __call__(self, ins):
        self.done += 1
        ins.then_inc(self.sem, 1)
        self.eng.wait_ge(self.sem, self.done)


PARTS2 = ((0, 0), (0, 1), (1, 0))
DOWN_LAG = 2
TURN_AT = 3


def ffn_phase(nc, m, name, d, x_in, x_out):
    with ExitStack() as ctx:
        def sem(what):
            return ctx.enter_context(nc.semaphore(f"{name}_{what}"))

        def sb(what, cols, dt=F32):
            return ctx.enter_context(nc.sbuf_tensor(f"{name}_{what}_s", [P, cols], dt))[:, :]

        x_n = sb("x_n", NT * C).rearrange("p (n c) -> p n c", n=NT)
        xT = [sb(f"xT_{k}", NT * P, F32R) for k in ("high", "low")]
        wT = sb("wT", NT * P, BF16)
        sig = sb("sigmoid", NT * 24).rearrange("p (n e) -> p n e", n=NT)
        rep = sb("replaced", NT * 24).rearrange("p (n e) -> p n e", n=NT)
        top = sb("top", NT * 8).rearrange("p (n e) -> p n e", n=NT)
        two = sb("two", NT * 8).rearrange("p (n e) -> p n e", n=NT)
        sums = sb("sums", NT)
        inv = sb("inv", NT)
        wts = sb("wts", NT * E).rearrange("p (n e) -> p n e", n=NT)
        parts = sb("parts", NT * 3 * E, BF16).rearrange("p (n k e) -> p n k e", n=NT, k=3)
        hid = [sb(f"hid{k}", SLAB) for k in range(3)]
        hid_parts = [[sb(f"hid_{k}{c}", SLAB, F32R) for c in range(NCH + 1)] for k in ("high", "low")]
        th = [m.v[:, s * SLAB:(s + 1) * SLAB] for s in range(3)]
        silu = [sb(f"silu{k}", SLAB) for k in range(3)]
        gated = m.vcur[:, 0:SLAB]
        out_sb = m.y[:, 0:SLAB]
        raw_sh, raw_sd, raw_route = m.y[:, 0:2 * I], m.y[:, P:P + C], m.y[:, 2 * P:2 * P + E]
        raws = [(m.v[:, :], m.w_gu, 0, 2 * NCH * P), (raw_sh, m.w_gu, 2 * NCH * P, P),
                (m.vcur[:, :], m.w_dn, 0, NCH * C)]

        ps = m.ps
        bank = [ps[:, b * 512:(b + 1) * 512] for b in range(8)]
        gate_ps, up_ps, wt_ps = bank[0:2], bank[2:4], bank[4:6]
        shared_ps, out_ps = bank[6], bank[7]
        logit_ps = bank[7][:, 0:NT * E].rearrange("p (n e) -> p n e", n=NT)
        wT_ps = ps[0:3 * E, 4 * 512:6 * 512].bitcast(BF16)

        x_in_s, const_s, route_s, weights_s = sem("x_in"), sem("const"), sem("route"), sem("weights")
        high_s, low_s = sem("weights_high"), sem("weights_low")
        link_s = sem("link")
        ln = [link_s, sem("var"), sem("sd"), sem("xn"), sem("xt_psum"), sem("xt"), sem("xt_low")]
        xt_ready, xt_low = ln[5], ln[6]
        logits_s, z_s, tanh_s = sem("logits"), sem("z"), sem("tanh")
        parts_s, wt_psum_s, wt_s = sem("parts"), sem("wt_psum"), sem("wt")
        gate_s = sem("gate")
        up_s = sem("up")
        th_s = sem("tanh_gate")
        hid_s = sem("hidden")
        hidh_s, hidl_s = sem("hidden_high"), sem("hidden_low")
        down_s = sem("down")
        sum_s = sem("sum")
        turned_s = sem("turned")
        x_s = sem("x_new")
        store_s = sem("store")
        ln_vector, ln_low, ln_scalar, ln_tensor = layer_norm(m, x_n, xT[0], xT[1], ln)
        N = NCH + 1

        with nc.Block() as block:

            @block.sync
            def _(sp):
                if x_in is not None:
                    for s in range(2):
                        sp.dma_start(m.x[:, s * NT // 2:(s + 1) * NT // 2],
                                     x_in[:, s * NT // 2:(s + 1) * NT // 2]).then_inc(x_in_s, 16)
                    sp.dma_start(m.ident[:, :], d["identity"]).then_inc(const_s, 16)
                    sp.dma_start(raw_route, d["gate_w"]).then_inc(route_s, 16)
                    sp.dma_start(m.gate_b[:, :], d["gate_b"].partition_broadcast(P)).then_inc(route_s, 16)
                    sp.dma_start(m.ident_bf[:, :], d["identity_bf"]).then_inc(const_s, 16)
                    gate_up = m.v[:, :].rearrange("p (w e i) -> p w e i", w=2, e=E)
                    for w, key in enumerate(("experts_wg", "experts_wu")):
                        sp.dma_start(gate_up[:, w], d[key].rearrange("e d i -> d e i")).then_inc(weights_s, 16)
                    sp.dma_start(raw_sh[:, 0:I], d["shared_wg"]).then_inc(weights_s, 16)
                    sp.dma_start(raw_sh[:, I:2 * I], d["shared_wu"]).then_inc(weights_s, 16)
                    sp.dma_start(m.vcur[:, :].rearrange("p (c k) -> p c k", c=NCH),
                                 d["experts_wd"].rearrange("(c e) i d -> (e i) c d", e=2)).then_inc(weights_s, 16)
                    sp.dma_start(raw_sd[0:I], d["shared_wd"]).then_inc(weights_s, 16)
                    sp.dma_start(m.select[0:3 * E, :], d["select"]).then_inc(weights_s, 16)
                    sp.dma_start(m.q[ROWS_D:ROWS_1, :], d["q_bias"]).then_inc(m.bias_loaded, 16)
                    sp.dma_start(m.k[ROWS_D:ROWS_2, :].rearrange("p (h t) -> p h t", h=H),
                                 d["k_bias"].unsqueeze(1).to_broadcast([ROWS_B + 3, H, T])
                                 ).then_inc(m.bias_loaded, 16)
                if x_out is not None:
                    for s in range(NS):
                        sp.wait_ge(x_s, s + 1)
                        sp.dma_start(x_out[:, s * TPS:(s + 1) * TPS],
                                     m.x[:, s * TPS:(s + 1) * TPS]).then_inc(store_s, 16)
                    sp.wait_ge(store_s, 16 * NS)

            @block.gpsimd
            def _(pool):
                if x_in is not None:
                    pool.wait_ge(high_s, 1)
                    pool.tensor_tensor(m.w_gate[1][:, :], raw_route, m.w_gate[0][:, :].bitcast(F32),
                                       ALU.subtract).then_inc(low_s, 1)
                    for n, (raw, part, at, size) in enumerate(raws):
                        pool.wait_ge(high_s, n + 2)
                        pool.tensor_tensor(part[1][:, at:at + size], raw, part[0][:, at:at + size].bitcast(F32),
                                           ALU.subtract).then_inc(low_s, 1)
                    pool.wait_ge(high_s, len(raws) + 2)
                    pool.tensor_tensor(m.w_dn[1][0:I, NCH * C:N * C], raw_sd[0:I],
                                       m.w_dn[0][0:I, NCH * C:N * C].bitcast(F32),
                                       ALU.subtract).then_inc(low_s, 1)

                def slab(s, first):
                    for c in range(N):
                        n = s * N + c
                        rows = slice(0, P) if c < NCH else slice(0, I)
                        if not first:
                            pool.wait_ge(down_s, n - N + 1)
                        pool.wait_ge(hidh_s, n + 1)
                        pool.tensor_tensor(hid_parts[1][c][rows], hid[c % 3][rows],
                                           hid_parts[0][c][rows].bitcast(F32), ALU.subtract).then_inc(hidl_s, 1)

                slab(0, True)
                with pool.Fori(1, NS) as s:
                    slab(s, False)

            @block.scalar
            def _(act):
                if x_in is not None:
                    act.wait_ge(route_s, 32)
                    act.activation(m.w_gate[0][:, :], raw_route, ACT.Copy).then_inc(high_s, 1)
                ln_scalar(act)
                if x_in is not None:
                    act.wait_ge(weights_s, 16 * 7)
                    for raw, part, at, size in raws:
                        act.activation(part[0][:, at:at + size], raw, ACT.Copy).then_inc(high_s, 1)
                    act.activation(m.w_dn[0][0:I, NCH * C:N * C], raw_sd[0:I], ACT.Copy).then_inc(high_s, 1)
                act.wait_ge(z_s, 1)
                act.activation(wts, wts, ACT.Tanh, scale=0.5).then_inc(tanh_s, 1)
                for s in range(2):
                    act.wait_ge(wt_psum_s, s + 1)
                    act.activation(wT[0:3 * E, s * 1024:(s + 1) * 1024],
                                   wT_ps[:, s * 1024:(s + 1) * 1024], ACT.Copy).then_inc(wt_s, 1)

                def tanh(s, c):
                    act.wait_ge(gate_s, s * N + c + 1)
                    rows = slice(0, P) if c < NCH else slice(0, I)
                    gate = gate_ps[c % 2] if c < NCH else shared_ps[rows]
                    act.activation(th[c % 3][rows], gate, ACT.Tanh, scale=0.5).then_inc(th_s, 1)

                def high(s, c, first):
                    n = s * N + c
                    rows = slice(0, P) if c < NCH else slice(0, I)
                    if not first:
                        act.wait_ge(down_s, n - N + 1)
                    act.wait_ge(hid_s, n + 1)
                    act.activation(hid_parts[0][c][rows], hid[c % 3][rows], ACT.Copy).then_inc(hidh_s, 1)

                def sum_out(s):
                    act.wait_ge(down_s, (s + 1) * N)
                    if not isinstance(s, int) or s > 0:
                        act.wait_ge(turned_s, s)
                    act.activation(out_sb, out_ps, ACT.Copy).then_inc(sum_s, 1)

                def slab(s, first, last):
                    for c in range(N):
                        if c + 1 < N:
                            tanh(s, c + 1)
                        elif not last:
                            tanh(s + 1, 0)
                        if c == DOWN_LAG and not first:
                            sum_out(s - 1)
                        high(s, c, first)

                tanh(0, 0)
                slab(0, True, False)
                with act.Fori(1, NS - 1) as s:
                    slab(s, False, False)
                slab(NS - 1, False, True)
                sum_out(NS - 1)

            @block.vector
            def _(dve):
                link = Chain(dve, link_s)
                if x_in is not None:
                    dve.wait_ge(x_in_s, 32)
                ln_vector(dve, link)
                dve.memset(sig, -1.0)
                link(dve.memset(two, -1.0))
                ln_low(dve)
                link(dve.scalar_tensor_tensor(m.x, x_n, 0.5, m.x, ALU.mult, ALU.add))
                if x_in is not None:
                    dve.wait_ge(route_s, 32)
                dve.wait_ge(logits_s, 1)
                dve.tensor_tensor(wts, logit_ps, m.gate_b[:, :].unsqueeze(1).to_broadcast([P, NT, E]),
                                  ALU.add).then_inc(z_s, 1)
                dve.wait_ge(tanh_s, 1)
                link(dve.tensor_scalar(sig[:, :, 0:E], wts, 0.5, 0.5, ALU.mult, ALU.add))
                for n in range(NT):
                    ins = dve.max(top[:, n], sig[:, n, 0:E])
                link(ins)
                link(dve.tensor_copy(two[:, :, 0:2], top[:, :, 0:2]))
                for n in range(NT):
                    ins = dve.match_replace(rep[:, n], two[:, n], sig[:, n], 0.0)
                link(ins)
                dve.tensor_tensor(wts, sig[:, :, 0:E], rep[:, :, 0:E], ALU.subtract)
                link(dve.tensor_tensor(sums, top[:, :, 0], top[:, :, 1], ALU.add))
                link(dve.reciprocal(inv, sums))
                link(dve.tensor_tensor(wts, wts, inv.unsqueeze(2).to_broadcast([P, NT, E]), ALU.mult))
                link(dve.tensor_copy(parts[:, :, 0], wts))
                link(dve.tensor_tensor(wts, wts, parts[:, :, 0], ALU.subtract))
                link(dve.tensor_copy(parts[:, :, 1], wts))
                dve.tensor_tensor(parts[:, :, 2], wts, parts[:, :, 1], ALU.subtract).then_inc(parts_s, 1)
                base = link.done

                def chunk(s, c):
                    n = s * N + c
                    k = base + s * (2 * NCH + 1) + 2 * c
                    dve.wait_ge(th_s, n + 1)
                    shared = c == NCH
                    rows = slice(0, I) if shared else slice(0, P)
                    gate = shared_ps[rows] if shared else gate_ps[c % 2]
                    dve.scalar_tensor_tensor(silu[c % 3][rows], th[c % 3][rows], 1.0, gate,
                                             ALU.add, ALU.mult).then_inc(link_s, 1)
                    dve.wait_ge(link_s, k + 1)
                    if not isinstance(s, int) or n >= 3:
                        dve.wait_ge(hidl_s, n - 2)
                    if shared:
                        dve.scalar_tensor_tensor(hid[c % 3][rows], silu[c % 3][rows], 0.25, shared_ps[I:2 * I],
                                                 ALU.mult, ALU.mult).then_inc(hid_s, 1)
                        return
                    dve.wait_ge(up_s, s * NCH + c + 1)
                    dve.tensor_tensor(gated, silu[c % 3], up_ps[c % 2], ALU.mult).then_inc(link_s, 1)
                    dve.wait_ge(link_s, k + 2)
                    dve.tensor_tensor(hid[c % 3], gated, wt_ps[c % 2], ALU.mult).then_inc(hid_s, 1)

                def update(s):
                    dve.wait_ge(turned_s, s + 1)
                    xs = m.x[:, bass.ts(s, TPS)]
                    dve.tensor_tensor(xs, shared_ps.rearrange("p (n c) -> p n c", n=TPS), xs,
                                      ALU.add).then_inc(x_s, 1)

                def slab(s, first):
                    for c in range(N):
                        chunk(s, c)
                        if c == TURN_AT + 1 and not first:
                            update(s - 1)

                slab(0, True)
                with dve.Fori(1, NS) as s:
                    slab(s, False)
                update(NS - 1)

            @block.tensor
            def _(pe):
                if x_in is not None:
                    pe.wait_ge(const_s, 32)
                ln_tensor(pe)
                if x_in is not None:
                    pe.wait_ge(low_s, 1)
                for n in range(NT):
                    if n % TPS == 0:
                        pe.wait_ge(xt_low, n // TPS + 1)
                    for k, (a, b) in enumerate(PARTS2):
                        ins = pe.matmul(logit_ps[:, n], xT[b][:, n * P:(n + 1) * P], m.w_gate[a][:, :],
                                        start=(k == 0), stop=(k == 2))
                ins.then_inc(logits_s, 1)
                pe.wait_ge(parts_s, 1)
                for n in range(NT):
                    ins = pe.transpose(wT_ps[:, n * P:(n + 1) * P],
                                       parts[:, n].rearrange("p k e -> p (k e)"), m.ident_bf[:, :])
                    if n % (NT // 2) == NT // 2 - 1:
                        ins.then_inc(wt_psum_s, 1)

                def product(out, n_weights, s):
                    for k, (a, b) in enumerate(PARTS2):
                        ins = pe.matmul(out, m.w_gu[a][:, n_weights * P:(n_weights + 1) * P],
                                        xT[b][:, bass.ts(s, SLAB)], start=(k == 0), stop=(k == 2))
                    return ins

                def products(s, c):
                    if c == NCH:
                        product(shared_ps, 2 * NCH, s).then_inc(gate_s, 1)
                        return
                    product(gate_ps[c % 2], c, s).then_inc(gate_s, 1)
                    product(up_ps[c % 2], NCH + c, s)
                    pe.matmul(wt_ps[c % 2], m.select[0:3 * E, c * P:(c + 1) * P],
                              wT[0:3 * E, bass.ts(s, SLAB)], start=True, stop=True).then_inc(up_s, 1)

                def down(s, c):
                    pe.wait_ge(hidl_s, s * N + c + 1)
                    rows = slice(0, P) if c < NCH else slice(0, I)
                    for k, (a, b) in enumerate(PARTS2):
                        ins = pe.matmul(out_ps, m.w_dn[a][rows, c * C:(c + 1) * C], hid_parts[b][c][rows],
                                        start=(c == 0 and k == 0), stop=(c == NCH and k == 2),
                                        skip_group_check=True)
                    ins.then_inc(down_s, 1)

                def turn(s):
                    pe.wait_ge(sum_s, s + 1)
                    for j in range(TPS):
                        ins = pe.transpose(shared_ps[:, j * P:(j + 1) * P], out_sb[:, j * P:(j + 1) * P],
                                           m.ident[:, :])
                    ins.then_inc(turned_s, 1)

                def slab(s, first, last):
                    for c in range(N):
                        nxt = c + 2
                        if nxt <= NCH:
                            if nxt < NCH:
                                pe.wait_ge(hid_s, s * N + nxt - 1)
                            elif not first:
                                pe.wait_ge(x_s, s)
                            products(s, nxt)
                        elif not last:
                            pe.wait_ge(hid_s, s * N + NCH - 1 + nxt - N)
                            products(s + 1, nxt - N)
                        if c >= DOWN_LAG:
                            if c == DOWN_LAG and not first:
                                pe.wait_ge(sum_s, s)
                            down(s, c - DOWN_LAG)
                        elif not first:
                            down(s - 1, c - DOWN_LAG + N)
                        if c == TURN_AT and not first:
                            turn(s - 1)

                if x_in is not None:
                    pe.wait_ge(low_s, len(raws) + 2)
                pe.wait_ge(wt_s, 2)
                for c in range(2):
                    products(0, c)
                slab(0, True, False)
                with pe.Fori(1, NS - 1) as s:
                    slab(s, False, False)
                slab(NS - 1, False, True)
                for c in range(N - DOWN_LAG, N):
                    down(NS - 1, c)
                turn(NS - 1)


ROW_INCS = 16 * 2 * len(RUNS)


def store_q(eng, scratch, parts, b, n, done):
    for k in range(3):
        to = scratch[b, 0, k].rearrange("c t -> (c t)").rearrange(
            "(e g n j t) -> n (e g) j t", e=DH, g=H // GH, n=2, j=GH)[n]
        eng.dma_start(to, parts[:, b, 0, k, n * SLAB:(n + 1) * SLAB]).then_inc(done, 16)


def load_rows(eng, m, scratch, b, g, groups, done):
    size = groups * GH * T
    at = g * GH * T
    for w, rows in enumerate((m.q, m.k)):
        parts = scratch[b, w].rearrange("k (e g) c -> k e (g c)", e=DH)[:, :, at:at + size]
        for lo, hi in RUNS:
            first, step = SPLIT[lo][w], SPLIT[lo + 1][w] - SPLIT[lo][w] if hi - lo > 1 else 1
            assert [x[w] for x in SPLIT[lo:hi]] == [first + step * n for n in range(hi - lo)]
            if step:
                source = parts[first:first + hi - lo]
            else:
                source = parts[first].unsqueeze(0).to_broadcast([hi - lo, DH, size])
            eng.dma_start(rows[lo * DH:hi * DH, at:at + size], source).then_inc(done, 16)


def qkv_phase(nc, m, d, scratch):
    with ExitStack() as ctx:
        def sem(what):
            return ctx.enter_context(nc.semaphore(f"qkv_{what}"))

        def sb(what, cols, dt=F32):
            return ctx.enter_context(nc.sbuf_tensor(f"qkv_{what}_s", [P, cols], dt))[:, :]

        x_n = sb("x_n", NT * C).rearrange("p (n c) -> p n c", n=NT)
        xT = sb("xT", NT * P)
        parts = sb("parts", B * 2 * 3 * T, BF16).rearrange("p (b w k t) -> p b w k t", b=B, w=2, k=3)
        w_qkv = m.vcur[:, 0:3 * C]
        b_v = m.vcur[:, 3 * C:4 * C]
        w_qk = m.vcur[:, 4 * C:6 * C]
        rest = [m.y[:, 0:SLAB], m.y[:, SLAB:2 * SLAB]]
        v = m.v[:, :].rearrange("p (b g t k) -> p b g t k", b=B, g=H // GH, t=TB)
        bank = [m.ps[:, b * 512:(b + 1) * 512] for b in range(8)]
        qk_ps = bank[4:8] + bank[0:4]
        v_ps = bank[4:8]

        link_s = sem("link")
        ln = [link_s, sem("var"), sem("sd"), sem("xn"), sem("xt_psum"), sem("xt"), None]
        xt_ready = ln[5]
        w_s, w_qk_s, qk_s, v_s = sem("weights"), sem("qk_columns"), sem("qk_psum"), sem("v_psum")
        full_s = sem("full")
        p1_s, r1_s, p2_s, p3_s = sem("part1"), sem("rest1"), sem("part2"), sem("part3")
        vdone_s = sem("v_sbuf")
        stored = [sem(f"stored{b}") for b in range(B)]
        ln_vector, _, ln_scalar, ln_tensor = layer_norm(m, x_n, xT, None, ln)
        w_incs = 16 * 3
        order = [(s, w) for s in range(NS) for w in range(2)]

        def part(s, w, k):
            b, at = s * SLAB // T, s * SLAB % T
            return parts[:, b, w, k, at:at + SLAB]

        with nc.Block() as block:

            @block.sync
            def _(sp):
                sp.dma_start(w_qkv, d["W_qkv"]).then_inc(w_s, 16)
                sp.dma_start(b_v, d["b_qkv"][2 * C:3 * C].partition_broadcast(P)).then_inc(w_s, 16)
                sp.dma_start(m.b_qk[:, :], d["b_qk"]).then_inc(w_s, 16)
                for h in range(2):
                    sp.dma_start(m.decay[h][:, :], d["decay"][:, 0:GH * P]).then_inc(m.decay_loaded[h], 16)
                for b in range(B):
                    for n in range(2):
                        sp.wait_ge(p3_s, 2 * (2 * b + n) + 1)
                        store_q(sp, scratch, parts, b, n, stored[b])
                    sp.wait_ge(p3_s, 4 * (b + 1))
                    sp.dma_start(scratch[b, 1].rearrange("k c t -> c k t"), parts[:, b, 1]).then_inc(stored[b], 16)
                    if b == 0:
                        sp.wait_ge(stored[b], 16 * 7)
                        load_rows(sp, m, scratch, 0, 0, 1, m.rows_0)
                        load_rows(sp, m, scratch, 0, 1, 1, m.rows)
                        load_rows(sp, m, scratch, 0, 2, H // GH - 2, m.rows)
                sp.wait_ge(stored[1], 16 * 7)
                sp.dma_start(m.w_proj[:, :], d["W_proj"]).then_inc(m.proj_loaded, 16)
                sp.dma_start(m.b_proj[:, :], d["b_proj"].partition_broadcast(P)).then_inc(m.proj_loaded, 16)

            @block.scalar
            def _(act):
                ln_scalar(act)
                for n, (s, w) in enumerate(order):
                    act.wait_ge(full_s, n + 1)
                    act.activation(part(s, w, 0), rest[n % 2], ACT.Copy).then_inc(p1_s, 1)
                    act.wait_ge(r1_s, n + 1)
                    act.activation(part(s, w, 1), rest[n % 2], ACT.Copy).then_inc(p2_s, 1)

            @block.gpsimd
            def _(pool):
                pool.wait_ge(w_s, w_incs)
                pool.tensor_copy(w_qk.rearrange("p (w e h) -> p w h e", w=2, e=DH),
                                 w_qkv[:, 0:2 * C].rearrange("p (w h e) -> p w h e", w=2, e=DH)).then_inc(w_qk_s, 1)
                for n, (s, w) in enumerate(order):
                    pool.wait_ge(p2_s, n + 1)
                    pool.tensor_tensor(part(s, w, 2), rest[n % 2], part(s, w, 1), ALU.subtract).then_inc(p3_s, 1)

            @block.vector
            def _(dve):
                link = Chain(dve, link_s)
                ln_vector(dve, link)
                dve.wait_ge(w_s, w_incs)

                def full(n):
                    s, w = order[n]
                    dve.wait_ge(qk_s, n + 1)
                    if n >= 2:
                        dve.wait_ge(p3_s, n - 1)
                    dve.tensor_scalar(rest[n % 2], qk_ps[n], m.b_qk[:, w:w + 1], SCALE if w == 0 else 1.0,
                                      ALU.add, ALU.mult).then_inc(full_s, 1)

                full(0)
                for n, (s, w) in enumerate(order):
                    if n + 1 < len(order):
                        full(n + 1)
                    dve.wait_ge(p1_s, n + 1)
                    dve.tensor_tensor(rest[n % 2], rest[n % 2], part(s, w, 0), ALU.subtract).then_inc(r1_s, 1)
                for n in range(NT):
                    b, t = divmod(n, TB)
                    if n % TPS == 0:
                        dve.wait_ge(v_s, n // TPS + 1)
                    dve.tensor_tensor(v[:, b, :, t], v_ps[n // TPS][:, n % TPS * P:(n % TPS + 1) * P].rearrange(
                        "p (g k) -> p g k", g=H // GH), b_v.rearrange("p (g k) -> p g k", g=H // GH),
                        ALU.add).then_inc(vdone_s, 1)

            @block.tensor
            def _(pe):
                ln_tensor(pe)
                pe.wait_ge(xt_ready, NS)
                pe.wait_ge(w_s, w_incs)
                pe.wait_ge(w_qk_s, 1)
                for n, (s, w) in enumerate(order):
                    pe.matmul(qk_ps[n], w_qk[:, w * C:(w + 1) * C], xT[:, s * SLAB:(s + 1) * SLAB],
                              start=True, stop=True).then_inc(qk_s, 1)
                for n in range(NT):
                    if n % TPS == 0:
                        pe.wait_ge(full_s, n // TPS + 1)
                    ins = pe.matmul(v_ps[n // TPS][:, n % TPS * P:(n % TPS + 1) * P], xT[:, n * P:(n + 1) * P],
                                    w_qkv[:, 2 * C:3 * C], start=True, stop=True)
                    if n % TPS == TPS - 1:
                        ins.then_inc(v_s, 1)


QUADS = 2 * TB
UNITS = QUADS * GH
TILES = GH * TB
HALF = TILES // 2
AHEAD = TILES // 2 + 6
LAG = 2
SLOTS = 4
TURN = 3


def quad(q):
    n, s = divmod(q, TB)
    return (s + n * TB // 2) % TB, n


def has_diagonal(q):
    s, n = quad(q)
    return s // (TB // 2) == n


def tile_of(b):
    return (0, AHEAD + b) if b < TILES - AHEAD else (1, b - (TILES - AHEAD))


def tile_place(t):
    h, r = divmod(t, HALF)
    j, i = divmod(r, TB // 2)
    return h, j, h * (TB // 2) + i


LAST_TILE = (TILES - AHEAD - 1, TILES - AHEAD + HALF - 1)


def double_uses():
    uses = []
    for q in range(QUADS):
        if q == TURN:
            uses.append(("result", 1))
        if q == TURN + TB:
            uses.append(("result", 0))
        for b in (2 * q, 2 * q + 1):
            uses.append(("tile", b))
            if b == LAST_TILE[0] + 2:
                uses.append(("maxima", 1))
            if b == LAST_TILE[1] + 2:
                uses.append(("maxima", 0))
    return uses


BODY_USES = double_uses()
BEFORE_USES = [x for x in BODY_USES if x == ("maxima", 0) or (x[0] == "tile" and x[1] >= TILES - AHEAD)]
FIRST_USES = [x for x in BODY_USES if x != ("result", 1)]
LAST_USES = [x for x in BODY_USES if x not in BEFORE_USES] + [("result", "end")]


def use(g, what):
    if isinstance(g, int) and g < 1:
        return BEFORE_USES.index(what) if g < 0 else len(BEFORE_USES) + FIRST_USES.index(what)
    order = LAST_USES if isinstance(g, int) and g == NG - 1 else BODY_USES
    return g * len(BODY_USES) + (len(BEFORE_USES) - 1) + order.index(what)


def turn_of(g, what):
    return use(g if isinstance(g, int) else 2, what) % 2


def key_order(i):
    half = TB // 2
    own = [i // half * half + r for r in range(half)]
    other = [s for s in range(TB) if s not in own]
    if i % half < half // 2:
        at = i % half
        return own[at:] + own[:at] + other, 0
    at = i % half + 1
    return other + own[at:] + own[:at], TB - 1


def attention_phase(nc, m, d, scratch):
    assert len(BODY_USES) % 2 == 0
    with ExitStack() as ctx:
        def sem(what):
            return ctx.enter_context(nc.semaphore(f"att_{what}"))

        def sb(what, cols, dt=F32):
            return ctx.enter_context(nc.sbuf_tensor(f"att_{what}_s", [P, cols], dt))[:, :]

        probs = sb("probs", SLOTS * GH * SLAB).rearrange("p (s j t) -> p s j t", s=SLOTS, j=GH)
        decay_exp = sb("decay_exp", GH * P)
        v_group = m.vcur[:, :].rearrange("p (t j k) -> p t j k", t=TB, j=GH)
        double = [m.ps[:, 0:1024], m.ps[:, 1024:2048]]
        score_ps = [m.ps[:, 2048:2560], m.ps[:, 2560:3072]]
        acc_ps = m.ps[:, 3072:4096]
        parts = m.max_parts[:, :].rearrange("p (k h n) -> p h k n", k=3, h=2)
        recip = m.recip[:, :].rearrange("p (h t j) -> p h t j", h=2, t=TB // 2)

        vinit_s = sem("v_init")
        exp_table_s = sem("decay_exp")
        d_ready_s = sem("double_ready")
        d_free_s = sem("double_free")
        link_s = sem("link")
        recip_s = sem("recip")
        top_s = sem("maxima")
        parts_s = sem("max_parts")
        rows_s = sem("max_rows")
        score_s = sem("scores")
        exp_s = sem("exp")
        decay_s = sem("decayed")
        pv_s = sem("pv")
        y_s = sem("y")
        vg_s = sem("v_group")

        def q_cols(base, half, j, start, size):
            return bass.ds(base + (half * GH + j) * SLAB + start, size)

        def k_cols(base, j, start, size):
            return bass.ds(base + j * T + start, size)

        def base_of(g):
            return (g & 3) * (GH * T)

        with nc.Block() as block:

            @block.sync
            def _(sp):
                def rows(g, h, body):
                    sp.wait_ge(d_free_s, use(body, ("maxima", h)) + 1)
                    for k in range(3):
                        sp.dma_start(m.q[ROWS_1 + k:ROWS_1 + k + 1, q_cols(base_of(g), h, 0, 0, GH * SLAB)].rearrange(
                            "o (n t) -> o n t", n=HALF), m.max_rows[k * TILES + h * HALF:k * TILES + (h + 1) * HALF, :]
                        ).then_inc(rows_s, 16)

                def table(h, g):
                    sp.dma_start(m.decay[h][:, :], table_of("decay", g)).then_inc(m.decay_loaded[h], 16)

                def table_of(name, g):
                    return d[name][:, bass.ds(g * (GH * P), GH * P)]

                sp.dma_start(decay_exp, table_of("decay_exp", 0)).then_inc(exp_table_s, 16)
                rows(0, 0, -1)
                table(0, 1)
                for g in range(NG):
                    if 1 <= g <= NG - H // GH:
                        sp.wait_ge(m.rows, ROW_INCS * (g + 1))
                        sp.wait_ge(score_s, g * UNITS)
                        load_rows(sp, m, scratch, 1, g - 1, 1, m.rows)
                    rows(g, 1, g)
                    if g == NG - 1:
                        break
                    table(1, g + 1)
                    sp.wait_ge(decay_s, (g + 1) * TB)
                    sp.dma_start(decay_exp, table_of("decay_exp", g + 1)).then_inc(exp_table_s, 16)
                    rows(g + 1, 0, g)
                    if g < NG - 2:
                        table(0, g + 2)

            @block.gpsimd
            def _(pool):
                pool.memset(m.vcur[:, :], 0.0).then_inc(vinit_s, 1)
                pool.wait_ge(vinit_s, 1)
                pool.memset(v_group[:, :, :, DH:DH + 1], 1.0).then_inc(vinit_s, 1)
                pool.memset(m.max_parts[:, :], 0.0).then_inc(vinit_s, 1)
                pool.wait_ge(vinit_s, 3)

                def split(g, h):
                    top = m.max_a[:, h * HALF:(h + 1) * HALF]
                    rest = m.max_b[:, h * HALF:(h + 1) * HALF]
                    pool.wait_ge(top_s, 2 * g + h + 1)
                    pool.tensor_tensor(parts[:, h, 1], top, parts[:, h, 0], ALU.subtract)
                    pool.tensor_tensor(rest, top, parts[:, h, 0], ALU.subtract).then_inc(link_s, 1)
                    pool.wait_ge(link_s, 2 * g + h + 1)
                    pool.tensor_tensor(parts[:, h, 2], rest, parts[:, h, 1], ALU.subtract).then_inc(parts_s, 1)

                def body(g, first, last):
                    pool.wait_ge(exp_table_s, 16 * (g + 1))
                    for q in range(QUADS):
                        if q == (LAST_TILE[0] + 1) // 2:
                            split(g, 1)
                        if q == (LAST_TILE[1] + 1) // 2 and not last:
                            split(g + 1, 0)
                        if q == 1:
                            if not first:
                                pool.wait_ge(pv_s, g * QUADS)
                            pool.tensor_copy(v_group[:, :, :, 0:DH], m.v[:, bass.ts(g, TB * GH * DH)].rearrange(
                                "p (t j k) -> p t j k", t=TB, j=GH)).then_inc(vg_s, 1)
                        if not has_diagonal(q):
                            continue
                        pool.wait_ge(exp_s, g * UNITS + (q + 1) * GH)
                        at = quad(q)[0] % (TB // 2) * P
                        block_ = probs[:, q % SLOTS, :, at:at + P]
                        pool.tensor_tensor(block_, block_, decay_exp.rearrange("p (j t) -> p j t", j=GH),
                                           ALU.mult).then_inc(decay_s, 1)

                split(0, 0)
                body(0, True, False)
                with pool.Fori(1, NG - 1) as g:
                    body(g, False, False)
                body(NG - 1, False, True)

            @block.scalar
            def _(act):
                def result(g, h):
                    act.wait_ge(pv_s, g * QUADS + (h + 1) * TB)
                    act.activation(m.y[:, h * SLAB:(h + 1) * SLAB], acc_ps[:, h * SLAB:(h + 1) * SLAB],
                                   ACT.Copy).then_inc(y_s, 1)

                def body(g, first):
                    for q in range(QUADS):
                        if not first or q >= SLOTS:
                            act.wait_ge(pv_s, g * QUADS + q - SLOTS + 1)
                        for j in range(GH):
                            u = q * GH + j
                            act.wait_ge(score_s, g * UNITS + u + 1)
                            act.activation(probs[:, q % SLOTS, j], score_ps[u % 2], ACT.Exp).then_inc(exp_s, 1)
                        if q == LAG - 1 and not first:
                            result(g - 1, 1)
                        if q == TB + LAG - 1:
                            result(g, 0)

                body(0, True)
                with act.Fori(1, NG) as g:
                    body(g, False)
                result(NG - 1, 1)

            @block.vector
            def _(dve):
                def tile(g, b):
                    ahead, t = tile_of(b)
                    h, j, i = tile_place(t)
                    u = use(g, ("tile", b))
                    dve.wait_ge(d_ready_s, u + 1)
                    turn = turn_of(g, ("tile", b))
                    ps = double[turn]
                    if t % HALF == 0:
                        dve.wait_ge(m.decay_loaded[h], 16 * (g + ahead + 1))
                    if not isinstance(u, int) or u > 1:
                        dve.wait_ge(d_free_s, u - 1)
                    at = key_order(i)[1]
                    dve.tensor_reduce(m.max_a[:, t:t + 1], ps[:, P:T] if at == 0 else ps[:, 0:T - P], AX_X, ALU.max)
                    dve.tensor_tensor_reduce(
                        m.junk[:, turn * P:(turn + 1) * P], ps[:, at * P:(at + 1) * P],
                        m.decay[h][:, j * P:(j + 1) * P], 1.0, -3.0e38, ALU.add, ALU.max,
                        m.max_b[:, t:t + 1]).then_inc(d_free_s, 1)

                def top(g, h, body):
                    dve.wait_ge(d_free_s, use(body, ("tile", LAST_TILE[1 - h])) + 1)
                    half = slice(h * HALF, (h + 1) * HALF)
                    dve.tensor_tensor(parts[:, h, 0], m.max_a[:, half], m.max_b[:, half], ALU.max)
                    dve.tensor_tensor(m.max_a[:, half], m.max_a[:, half], m.max_b[:, half], ALU.max).then_inc(top_s, 1)

                def maxima(g, h, body):
                    what = ("maxima", h)
                    dve.wait_ge(d_ready_s, use(body, what) + 1)
                    if not (isinstance(g, int) and g == 0 and h == 0):
                        dve.wait_ge(rows_s, 48 * (2 * g + h))
                    dve.tensor_copy(m.max_rows[0:3 * TILES, :], double[turn_of(body, what)][
                        0:3 * TILES, 0:P // 2].bitcast(BF16)).then_inc(d_free_s, 1)

                def result(g, h, body, what):
                    dve.wait_ge(d_ready_s, use(body, what) + 1)
                    if not isinstance(g, int) or g > 0:
                        dve.wait_ge(d_free_s, use(body, what))
                    ps = double[turn_of(body, what)][:, 0:SLAB].rearrange("p (t j k) -> p t j k", t=TB // 2, j=GH)
                    dve.reciprocal(recip[:, h], ps[:, :, :, DH]).then_inc(recip_s, 1)
                    dve.wait_ge(recip_s, 2 * g + h + 1)
                    dve.tensor_tensor(m.v[:, bass.ts(g, TB * GH * DH)].rearrange(
                        "p (h t j k) -> p h t j k", h=2, t=TB // 2, j=GH)[:, h],
                        ps[:, :, :, 0:DH], recip[:, h].unsqueeze(3).to_broadcast([P, TB // 2, GH, DH]),
                        ALU.mult).then_inc(d_free_s, 1)

                def body(g, uses):
                    for kind, which in uses:
                        if kind == "result":
                            result(g - which, which, g, (kind, which))
                        elif kind == "maxima":
                            maxima(g + 1 - which, which, g)
                        else:
                            tile(g, which)
                            if which in LAST_TILE:
                                h = 1 - LAST_TILE.index(which)
                                top(g + 1 - h, h, g)

                dve.wait_ge(vinit_s, 3)
                body(-1, BEFORE_USES)
                body(0, FIRST_USES)
                with dve.Fori(1, NG - 1) as g:
                    body(g, BODY_USES)
                body(NG - 1, LAST_USES[:-1])
                result(NG - 1, 1, NG - 1, LAST_USES[-1])

            @block.tensor
            def _(pe):
                def double_free(g, what):
                    u = use(g, what)
                    if not isinstance(u, int) or u > 1:
                        pe.wait_ge(d_free_s, u - 1)

                def tile(g, b, bank, base):
                    ahead, t = tile_of(b)
                    h, j, i = tile_place(t)
                    if bank == 0:
                        double_free(g, ("tile", b))
                    order = key_order(i)[0]
                    at, end = bank * TB // 2, (bank + 1) * TB // 2
                    while at < end:
                        size = 1
                        while at + size < end and order[at + size] == order[at] + size:
                            size += 1
                        ins = pe.matmul(double[turn_of(g, ("tile", b))][:, at * P:(at + size) * P],
                                        m.q[0:ROWS_1, q_cols(base[ahead], h, j, i % (TB // 2) * P, P)],
                                        m.k[0:ROWS_1, k_cols(base[ahead], j, order[at] * P, size * P)],
                                        start=True, stop=True)
                        at += size
                    if bank == 1:
                        ins.then_inc(d_ready_s, 1)

                def maxima(g, h, body):
                    double_free(body, ("maxima", h))
                    pe.wait_ge(parts_s, 2 * g + h + 1)
                    pe.transpose(double[turn_of(body, ("maxima", h))][0:3 * TILES, 0:P // 2].bitcast(BF16),
                                 m.max_parts[:, :], m.ident_bf[:, :]).then_inc(d_ready_s, 1)

                def result(g, h, body, what):
                    double_free(body, what)
                    pe.wait_ge(y_s, 2 * g + h + 1)
                    for t in range(TB // 2):
                        ins = pe.transpose(double[turn_of(body, what)][:, t * P:(t + 1) * P],
                                           m.y[:, h * SLAB + t * P:h * SLAB + (t + 1) * P], m.ident[:, :])
                    ins.then_inc(d_ready_s, 1)

                def scores(g, q, j, base):
                    u = q * GH + j
                    s, n = quad(q)
                    if not isinstance(g, int) or g > 0 or u >= 2:
                        pe.wait_ge(exp_s, g * UNITS + u - 1)
                    pe.matmul(score_ps[u % 2], m.k[0:ROWS_2, k_cols(base, j, s * P, P)],
                              m.q[0:ROWS_2, q_cols(base, n, j, 0, SLAB)],
                              start=True, stop=True).then_inc(score_s, 1)

                def pv(g, q):
                    s, n = quad(q)
                    if has_diagonal(q):
                        pe.wait_ge(decay_s, g * TB + sum(has_diagonal(x) for x in range(q + 1)))
                    else:
                        pe.wait_ge(exp_s, g * UNITS + (q + 1) * GH)
                    if q == 0:
                        pe.wait_ge(vg_s, g + 1)
                    if q % TB == 0 and (not isinstance(g, int) or g > 0):
                        pe.wait_ge(y_s, 2 * g - 1 + n)
                    for j in range(GH):
                        ins = pe.matmul(acc_ps[32 * j:32 * (j + 1), n * SLAB:(n + 1) * SLAB], v_group[:, s, j],
                                        probs[:, q % SLOTS, j], start=(q % TB == 0), stop=(q % TB == TB - 1),
                                        skip_group_check=True)
                    ins.then_inc(pv_s, 1)

                base_regs = [pe.alloc_register(f"base_{k}") for k in range(2)]

                def body(g, uses, first):
                    for q in range(QUADS):
                        if q % 4 == 0:
                            base = [base_of(g + ahead) for ahead in range(2)]
                            if not isinstance(g, int):
                                for k, x in enumerate(base):
                                    pe.reg_mov(base_regs[k], x)
                                base = [pe.snap(x, min_val=0, max_val=(H // GH - 1) * GH * T) for x in base_regs]
                        if q % TB == 0:
                            pe.wait_ge(rows_s, 48 * (2 * g + q // TB + 1))
                        if q == (TILES - AHEAD) // 2 and ("maxima", 0) in uses:
                            pe.wait_ge(m.rows, ROW_INCS * (2 if first else g))
                        h = 1 if q == TURN else 0
                        if q % TB == TURN and ("result", h) in uses:
                            result(g - h, h, g, ("result", h))
                        two = [("tile", b) in uses for b in (2 * q, 2 * q + 1)]
                        scores(g, q, 0, base[0])
                        if two[0]:
                            tile(g, 2 * q, 0, base)
                        scores(g, q, 1, base[0])
                        if two[0]:
                            tile(g, 2 * q, 1, base)
                        if two[1]:
                            tile(g, 2 * q + 1, 0, base)
                        scores(g, q, 2, base[0])
                        if two[1]:
                            tile(g, 2 * q + 1, 1, base)
                        scores(g, q, 3, base[0])
                        if q >= LAG:
                            pv(g, q - LAG)
                        elif not first:
                            pv(g - 1, QUADS - LAG + q)
                        for h in range(2):
                            if ("maxima", h) in uses and LAST_TILE[1 - h] + 2 == 2 * q + 1:
                                maxima(g + 1 - h, h, g)

                pe.wait_ge(m.bias_loaded, 16 * 2)
                pe.wait_ge(m.rows_0, ROW_INCS)
                for kind, which in BEFORE_USES:
                    if kind == "tile":
                        for bank in range(2):
                            tile(-1, which, bank, (None, base_of(0)))
                    else:
                        maxima(0, 0, -1)
                body(0, FIRST_USES, True)
                with pe.Fori(1, NG - 1) as g:
                    body(g, BODY_USES, False)
                body(NG - 1, LAST_USES, False)
                for q in range(QUADS - LAG, QUADS):
                    pv(NG - 1, q)
                result(NG - 1, 1, NG - 1, LAST_USES[-1])


def project_phase(nc, m):
    with ExitStack() as ctx:
        def sem(what):
            return ctx.enter_context(nc.semaphore(f"proj_{what}"))

        yT = ctx.enter_context(nc.sbuf_tensor("yT_s", [P, NT * P], F32))[:, :]
        y = ctx.enter_context(nc.sbuf_tensor("y_tiles_s", [P, NT * P], F32))[:, :].rearrange(
            "p (b t g k) -> p b t g k", b=B, g=H // GH, t=TB)
        v = m.v[:, :].rearrange("p (b g t k) -> p b g t k", b=B, g=H // GH, t=TB)
        y_s, turned_s, yt_s, out_s, bias_s, x_s = sem("y"), sem("turned"), sem("yT"), sem("out"), sem("bias"), sem("x")

        with nc.Block() as block:

            @block.scalar
            def _(act):
                for s in range(NS):
                    act.wait_ge(turned_s, s + 1)
                    act.activation(yT[:, s * SLAB:(s + 1) * SLAB], m.ps[:, s * 512:(s + 1) * 512],
                                   ACT.Copy).then_inc(yt_s, 1)

            @block.vector
            def _(dve):
                for b in range(B):
                    dve.tensor_copy(y[:, b].rearrange("p t g k -> p g t k"), v[:, b]).then_inc(y_s, 1)
                dve.wait_ge(m.proj_loaded, 32)
                dve.tensor_tensor(m.x, m.x, m.b_proj[:, :].unsqueeze(1).to_broadcast([P, NT, C]),
                                  ALU.add).then_inc(bias_s, 1)
                dve.wait_ge(bias_s, 1)
                for s in range(NS):
                    dve.wait_ge(out_s, s + 1)
                    xs = m.x[:, s * TPS:(s + 1) * TPS]
                    dve.tensor_tensor(xs, m.ps[:, (4 + s) * 512:(5 + s) * 512].rearrange("p (n c) -> p n c", n=TPS),
                                      xs, ALU.add).then_inc(x_s, 1)
                dve.wait_ge(x_s, NS)

            @block.tensor
            def _(pe):
                for n in range(NT):
                    b, t = divmod(n, TB)
                    if t == 0:
                        pe.wait_ge(y_s, b + 1)
                    ins = pe.transpose(m.ps[:, n * P:(n + 1) * P], y[:, b, t].rearrange("p g k -> p (g k)"),
                                       m.ident[:, :])
                    if n % TPS == TPS - 1:
                        ins.then_inc(turned_s, 1)
                pe.wait_ge(m.proj_loaded, 32)
                for n in range(NT):
                    if n % TPS == 0:
                        pe.wait_ge(yt_s, n // TPS + 1)
                    ins = pe.matmul(m.ps[:, 2048 + n * P:2048 + (n + 1) * P], yT[:, n * P:(n + 1) * P],
                                    m.w_proj[:, :], start=True, stop=True)
                    if n % TPS == TPS - 1:
                        ins.then_inc(out_s, 1)


def build(nc, d, x_in, out, scratch):
    with ExitStack() as ctx:
        m = allocate(nc, ctx)
        ffn_phase(nc, m, "ffn1", d, x_in, None)
        qkv_phase(nc, m, d, scratch)
        attention_phase(nc, m, d, scratch)
        project_phase(nc, m)
        ffn_phase(nc, m, "ffn2", d, None, out)


_INS = ["L0_attn_x", "L0_attn_W_qkv", "L0_attn_b_qkv", "L0_attn_W_proj", "L0_attn_b_proj", "L0_ffn_gate_w",
        "L0_ffn_gate_b", "L0_ffn_shared_wg", "L0_ffn_shared_wu", "L0_ffn_shared_wd", "L0_ffn_experts_wg",
        "L0_ffn_experts_wu", "L0_ffn_experts_wd"]


def kernel(**inputs):
    import concourse.bacc as bacc
    from concourse.bass_utils import run_bass_kernel_spmd

    nc = bacc.Bacc("TRN2", target_bir_lowering=False, num_devices=1)
    arrays, d = {}, {}
    given = {k: np.ascontiguousarray(inputs[k]) for k in _INS}
    given["L0_attn_b_qk"] = np.ascontiguousarray(
        given["L0_attn_b_qkv"][:2 * C].reshape(2, H, DH).transpose(2, 1, 0).reshape(C, 2))
    for name, a in {**given, **constants()}.items():
        key = f"in_{name}_dram"
        arrays[key] = a
        short = name.replace("L0_ffn_", "").replace("L0_attn_", "")
        d[short] = nc.dram_tensor(key, a.shape, mybir.dt.from_np(a.dtype), kind="ExternalInput").ap()
    out = nc.dram_tensor("out_0_dram", (B, T, C), F32, kind="ExternalOutput").ap()
    tiled = "b (t p) c -> p (b t) c"
    scratch = nc.dram_tensor("parts_dram", (B, 2, 3, C, T), BF16, kind="Internal").ap()
    build(nc, d, d["x"].rearrange(tiled, p=P), out.rearrange(tiled, p=P), scratch)
    r = run_bass_kernel_spmd(nc, [arrays], core_ids=[0])
    return r.results[0]["out_0_dram"]
```

```python
from contextlib import ExitStack

import concourse.bass as bass
import numpy as np
from concourse import mybir

F32 = mybir.dt.float32
F32R = mybir.dt.float32r
BF16 = mybir.dt.bfloat16
ALU = mybir.AluOpType
ACT = mybir.ActivationFunctionType
AX_X = mybir.AxisListType.X

P = 128
B, T, C = 2, 1024, 128
H = 16
DH = C // H
NT = B * T // P
TB = T // P
E = 16
I = 64
NCH = E // 2
SLAB = 512
NS = B * T // SLAB
TPS = SLAB // P
EPS = 1e-5
GH = 4
NG = B * H // GH
SPLIT = ((0, 0), (0, 1), (0, 2), (1, 0), (1, 1), (2, 0))
RUNS = ((0, 3), (3, 5), (5, 6))
ROWS_D = len(SPLIT) * DH
ROWS_B = 2 * 3 * TB
ROWS_1 = ROWS_D + ROWS_B
ROWS_2 = ROWS_1 + 3
SCALE = float(DH) ** -0.5
VW = 32


def slopes():
    start = 2.0 ** (-(2.0 ** -(np.log2(H) - 3)))
    return np.array([start * start ** i for i in range(H)], np.float32)


def bf16_parts(a):
    parts, rest = [], np.asarray(a, np.float64)
    for _ in range(3):
        p = rest.astype(mybir.dt.np(BF16))
        parts.append(p)
        rest = rest - p.astype(np.float64)
    return parts


def constants():
    bf = mybir.dt.np(BF16)
    sl = slopes().astype(np.float64)
    pos = np.arange(T)
    blk = pos // P
    j = np.arange(TB)
    coef = (blk[None, :] > j[:, None]) + 0.5 * (blk[None, :] == j[:, None])
    away = pos[None, :] - P * j[:, None]
    here = (blk[None, :] == j[:, None]).astype(np.float64)
    q = np.zeros((ROWS_B, H, T), bf)
    for h in range(H):
        for p, part in enumerate(bf16_parts(sl[h] * coef)):
            q[p * TB:(p + 1) * TB, h] = part
        for p, part in enumerate(bf16_parts(-sl[h] * coef * away)):
            q[(3 + p) * TB:(4 + p) * TB, h] = part
    k = np.ones((ROWS_B + 3, T), bf)
    k[0:3 * TB] = np.tile(away * here, (3, 1)).astype(bf)
    k[3 * TB:6 * TB] = np.tile(here, (3, 1)).astype(bf)
    k[ROWS_B:] = -1
    d = np.abs(np.arange(P)[:, None] - np.arange(P)[None, :])
    table = (-0.5 * sl[None, :, None] * d[:, None, :])
    table = table[:, np.arange(NG * GH) % H]
    sel = np.zeros((3, E, NCH, 2, I), bf)
    for e in range(E):
        sel[:, e, e // 2, e % 2, :] = 0.25
    return {
        "identity": np.eye(P, dtype=np.float32),
        "identity_bf": np.eye(P).astype(bf),
        "select": sel.reshape(3 * E, NCH * P),
        "q_bias": np.ascontiguousarray(q.reshape(ROWS_B, H // GH, GH, 2, T // 2).swapaxes(2, 3)
                                       ).reshape(ROWS_B, H * T),
        "k_bias": k,
        "decay": table.reshape(P, -1).astype(np.float32),
        "decay_exp": np.exp(table).reshape(P, -1).astype(np.float32),
    }


TABLE = (2 * GH + 1) * P


def heads_of(table):
    return table[:, P:].rearrange("p (j k t) -> p j k t", j=GH, k=2)[:, :, 0]


class Mem:
    pass


def allocate(nc, ctx):
    m = Mem()

    def sb(name, cols, dt=F32, rows=P):
        return ctx.enter_context(nc.sbuf_tensor(name, [rows, cols], dt))

    m.x = sb("x", NT * C)[:, :].rearrange("p (n c) -> p n c", n=NT)
    m.q = sb("q_rows", H * T, BF16)
    m.k = sb("k_rows", H * T, BF16)
    m.w_gu = [sb(f"w_gate_up_{k}", (2 * NCH + 1) * P, F32R) for k in ("high", "low")]
    m.w_dn = [sb(f"w_down_{k}", (NCH + 1) * C, F32R) for k in ("high", "low")]
    m.w_gate = sb("w_route_parts", 2 * E, F32R)
    m.select = sb("select_s", NCH * P, BF16)
    m.v = sb("v_all", NG * TB * GH * DH)
    m.y = sb("y_group", T)
    m.vcur = sb("v_group", TB * GH * VW)
    m.ident = sb("identity_s", P)
    m.ident_bf = sb("identity_bf_s", P, BF16)
    m.gate_b = sb("gate_b_s", E)
    m.w_proj = sb("w_proj_s", C)
    m.b_proj = sb("b_proj_s", C)
    m.b_qk = sb("b_qk_s", 2)
    m.stats = sb("stats", NT * 6)
    m.mv = sb("mean_var", NT * 2)
    m.rs = sb("rstd", NT * 4)
    m.max_a = sb("max_off_diagonal", GH * TB)
    m.max_b = sb("max_diagonal", GH * TB)
    m.max_parts = sb("max_parts", 3 * GH * TB, BF16)
    m.max_rows = sb("max_rows", P, BF16)
    m.recip = sb("recip", TB * GH)
    m.bias_loaded = ctx.enter_context(nc.semaphore("bias_loaded"))
    m.rows_0 = ctx.enter_context(nc.semaphore("rows_of_group_0"))
    m.rows = ctx.enter_context(nc.semaphore("rows_of_later_groups"))
    m.stored = [[[ctx.enter_context(nc.semaphore(f"stored_{w}_{k}")) for k in range(3)] for w in "qk"],
                [ctx.enter_context(nc.semaphore(f"stored_{w}_late")) for w in "qk"]]
    m.decay_loaded = [ctx.enter_context(nc.semaphore(f"decay_loaded_{h}")) for h in range(2)]
    m.proj_loaded = ctx.enter_context(nc.semaphore("proj_loaded"))
    m.ps = ctx.enter_context(nc.psum_tensor("psum", [P, 8 * 512], F32))
    return m


def statistics(dve, m, tiles):
    for n in tiles:
        ins = dve.bn_stats(m.stats[:, 6 * n:6 * (n + 1)], m.x[:, n])
    return ins


def aggregate(dve, m, tiles):
    for n in tiles:
        ins = dve.bn_aggr(m.mv[:, 2 * n:2 * (n + 1)], m.stats[:, 6 * n:6 * (n + 1)])
    return ins


def inverse_deviation(m, tiles):
    rs = m.rs[:, :].rearrange("p (k n) -> p k n", k=4)
    var_eps, sd, r, t = (rs[:, k, tiles.start:tiles.stop] for k in range(4))
    mv = m.mv[:, :].rearrange("p (n c) -> p n c", n=NT)[:, tiles.start:tiles.stop]

    def variance(dve):
        return dve.tensor_scalar(var_eps, mv[:, :, 1], EPS, None, ALU.add)

    def root(act):
        return act.activation(sd, var_eps, ACT.Sqrt)

    def inverse(dve, link, beside=lambda k: None):
        link(dve.reciprocal(r, sd), lambda: beside(0))
        link(dve.scalar_tensor_tensor(t, var_eps, -0.5, r, ALU.mult, ALU.mult), lambda: beside(1))
        link(dve.tensor_tensor(t, t, r, ALU.mult))
        link(dve.scalar_tensor_tensor(sd, t, 1.5, r, ALU.add, ALU.mult))

    return variance, root, inverse


def layer_norm(m, x_n, xT, xT_low, sems, with_stats):
    link_sem, var_ready, sd_ready, xn_ready, xt_psum, xt_ready, low_ready = sems
    mv = m.mv[:, :].rearrange("p (n c) -> p n c", n=NT)
    sd = m.rs[:, NT:2 * NT]
    early = with_stats == NT
    variance, root, inverse = inverse_deviation(m, range((NS - 1) * TPS if early else 0, NT))

    def on_vector(dve, link, loaded=None):
        if with_stats < NT:
            if loaded is None:
                last = statistics(dve, m, range(with_stats, NT))
            else:
                for s in range(NS):
                    dve.wait_ge(loaded[s], 16)
                    last = statistics(dve, m, range(s * TPS, (s + 1) * TPS))
            link(last)

        def normalise(first, end):
            for n in range(first, end):
                dve.tensor_scalar(x_n[:, n], m.x[:, n], mv[:, n, 0:1], sd[:, n:n + 1],
                                  ALU.subtract, ALU.mult).then_inc(xn_ready, 1)

        if early:
            normalise(0, TPS)

        def beside(k):
            if early:
                normalise(TPS + k, TPS + k + 1)

        link(aggregate(dve, m, range((NS - 1) * TPS if with_stats else 0, NT)), lambda: beside(0))
        variance(dve).then_inc(var_ready, 1)
        beside(1)
        dve.wait_ge(sd_ready, 1)
        inverse(dve, link, lambda k: beside(2 + k))
        for s in range(NS):
            if not (early and s < 2):
                normalise(s * TPS, (s + 1) * TPS)
            if xT_low is not None and s > 0:
                low_on_vector(dve, s - 1)

    def low_on_vector(dve, s):
        cols = slice(s * SLAB, (s + 1) * SLAB)
        dve.wait_ge(xt_ready, s + 1)
        dve.tensor_tensor(xT_low[:, cols], m.ps[:, s * 512:(s + 1) * 512], xT[:, cols].bitcast(F32),
                          ALU.subtract).then_inc(low_ready, 1)

    def on_scalar(act, after=lambda s: None):
        act.wait_ge(var_ready, 1)
        root(act).then_inc(sd_ready, 1)
        for s in range(NS):
            act.wait_ge(xt_psum, s + 1)
            act.activation(xT[:, s * SLAB:(s + 1) * SLAB], m.ps[:, s * 512:(s + 1) * 512],
                           ACT.Copy).then_inc(xt_ready, 1)
            after(s)

    def on_tensor(pe, after=lambda s: None):
        for s in range(NS):
            for n in range(s * TPS, (s + 1) * TPS):
                pe.wait_ge(xn_ready, n + 1)
                last = pe.transpose(m.ps[:, n * P:(n + 1) * P], x_n[:, n], m.ident[:, :])
            last.then_inc(xt_psum, 1)
            if s > 0:
                after(s - 1)
        after(NS - 1)

    return on_vector, low_on_vector, on_scalar, on_tensor


class Chain:

    def __init__(self, eng, sem):
        self.eng, self.sem, self.done = eng, sem, 0

    def __call__(self, ins, beside=lambda: None):
        self.done += 1
        ins.then_inc(self.sem, 1)
        beside()
        self.eng.wait_ge(self.sem, self.done)


PARTS2 = ((0, 0), (0, 1), (1, 0))
DOWN_LAG = 2
TURN_AT = 3


def ffn_phase(nc, m, name, d, x_in, x_out, with_stats):
    with ExitStack() as ctx:
        def sem(what):
            return ctx.enter_context(nc.semaphore(f"{name}_{what}"))

        def sb(what, cols, dt=F32):
            return ctx.enter_context(nc.sbuf_tensor(f"{name}_{what}_s", [P, cols], dt))[:, :]

        x_n = sb("x_n", NT * C).rearrange("p (n c) -> p n c", n=NT)
        xT = [sb(f"xT_{k}", NT * P, F32R) for k in ("high", "low")]
        wT = sb("wT", NT * P, BF16)
        sig = sb("sigmoid", NT * 24).rearrange("p (n e) -> p n e", n=NT)
        rep = sb("replaced", NT * 24).rearrange("p (n e) -> p n e", n=NT)
        top = sb("top", NT * 8).rearrange("p (n e) -> p n e", n=NT)
        two = sb("two", NT * 8).rearrange("p (n e) -> p n e", n=NT)
        sums = sb("sums", NT)
        inv = sb("inv", NT)
        wts = sb("wts", NT * E).rearrange("p (n e) -> p n e", n=NT)
        parts = sb("parts", NT * 3 * E, BF16).rearrange("p (n k e) -> p n k e", n=NT, k=3)
        hid = [sb(f"hid{k}", SLAB) for k in range(3)]
        hid_parts = [[sb(f"hid_{k}{c}", SLAB, F32R) for c in range(NCH + 1)] for k in ("high", "low")]
        th = [m.v[:, s * SLAB:(s + 1) * SLAB] for s in range(3)]
        silu = [sb(f"silu{k}", SLAB) for k in range(3)]
        gated = m.vcur[:, 0:SLAB]
        out_sb = m.y[:, 0:SLAB]
        raw_sh, raw_sd, raw_route = m.y[:, 0:2 * I], m.y[:, P:P + C], m.y[:, 2 * P:2 * P + E]
        half_gu = NCH * P
        raws = [(m.v[:, 0:half_gu], m.w_gu, 0, P), (m.v[:, half_gu:2 * half_gu], m.w_gu, half_gu, P),
                (raw_sh, m.w_gu, 2 * half_gu, P), (m.vcur[:, :], m.w_dn, 0, P), (raw_sd, m.w_dn, NCH * C, I)]

        def raw_and_parts(n):
            raw, part, at, rows = raws[n]
            size = raw.shape[-1]
            return raw[0:rows], part[0][0:rows, at:at + size], part[1][0:rows, at:at + size]

        ps = m.ps
        bank = [ps[:, b * 512:(b + 1) * 512] for b in range(8)]
        gate_ps, up_ps, wt_ps = bank[0:2], bank[2:4], bank[4:6]
        shared_ps, out_ps = bank[6], bank[7]
        logit_ps = [bank[b][:, 0:NT * E].rearrange("p (n k e) -> p n k e", n=NT // 2, k=2) for b in (5, 7)]
        wT_ps = shared_ps[0:3 * E].bitcast(BF16)
        halves = [slice(h * NT // 2, (h + 1) * NT // 2) for h in range(2)]

        x_in_s = [sem(f"x_in_{s}") for s in range(NS)]
        const_s, route_s, select_s = sem("const"), sem("route"), sem("select")
        weights_s = [sem(f"weights_{n}") for n in range(len(raws))]
        high_s, low_s = sem("weights_high"), sem("weights_low")
        link_s = sem("link")
        ln = [link_s, sem("var"), sem("sd"), sem("xn"), sem("xt_psum"), sem("xt"), sem("xt_low")]
        xt_ready, xt_low = ln[5], ln[6]
        fill_s = sem("fillers")
        logits_s, z_s, tanh_s, chosen_s = sem("logits"), sem("z"), sem("tanh"), sem("chosen")
        route_link_s, parts_link_s = sem("route_link"), sem("parts_link")
        parts_s, wt_psum_s, wt_s = sem("parts"), sem("wt_psum"), sem("wt")
        half_s = sem("half")
        residual_s = sem("residual")
        gate_s = sem("gate")
        up_s, w_s = sem("up"), sem("w")
        th_s = sem("tanh_gate")
        hid_s = sem("hidden")
        hidh_s, hidl_s = sem("hidden_high"), sem("hidden_low")
        down_s = sem("down")
        sum_s = sem("sum")
        turned_s = sem("turned")
        x_s = sem("x_new")
        store_s = sem("store")
        stats_s = sem("stats")
        ln_vector, ln_low, ln_scalar, ln_tensor = layer_norm(m, x_n, xT[0], xT[1], ln, with_stats)
        N = NCH + 1

        with nc.Block() as block:

            @block.sync
            def _(sp):
                if x_in is not None:
                    for s in range(NS):
                        sp.dma_start(m.x[:, s * TPS:(s + 1) * TPS],
                                     x_in[:, s * TPS:(s + 1) * TPS]).then_inc(x_in_s[s], 16)
                    sp.dma_start(m.ident[:, :], d["identity"]).then_inc(const_s, 16)
                    sp.dma_start(raw_route, d["gate_w"]).then_inc(route_s, 16)
                    sp.dma_start(m.gate_b[:, :], d["gate_b"].partition_broadcast(P)).then_inc(route_s, 16)
                    sp.dma_start(m.ident_bf[:, :], d["identity_bf"]).then_inc(const_s, 16)
                    gate_up = m.v[:, :].rearrange("p (w e i) -> p w e i", w=2, e=E)
                    for w, key in enumerate(("experts_wg", "experts_wu")):
                        sp.dma_start(gate_up[:, w], d[key].rearrange("e d i -> d e i")).then_inc(weights_s[w], 16)
                    sp.dma_start(raw_sh[:, 0:I], d["shared_wg"]).then_inc(weights_s[2], 16)
                    sp.dma_start(raw_sh[:, I:2 * I], d["shared_wu"]).then_inc(weights_s[2], 16)
                    sp.dma_start(m.vcur[:, :].rearrange("p (c k) -> p c k", c=NCH),
                                 d["experts_wd"].rearrange("(c e) i d -> (e i) c d", e=2)).then_inc(weights_s[3], 16)
                    sp.dma_start(raw_sd[0:I], d["shared_wd"]).then_inc(weights_s[4], 16)
                    sp.dma_start(m.select[0:3 * E, :], d["select"]).then_inc(select_s, 16)
                    sp.dma_start(m.q[ROWS_D:ROWS_1, :], d["q_bias"]).then_inc(m.bias_loaded, 16)
                    sp.dma_start(m.k[ROWS_D:ROWS_2, :].rearrange("p (h t) -> p h t", h=H),
                                 d["k_bias"].unsqueeze(1).to_broadcast([ROWS_B + 3, H, T])
                                 ).then_inc(m.bias_loaded, 16)
                if x_out is not None:
                    for s in range(NS):
                        sp.wait_ge(x_s, s + 1)
                        sp.dma_start(x_out[:, s * TPS:(s + 1) * TPS],
                                     m.x[:, s * TPS:(s + 1) * TPS]).then_inc(store_s, 16)
                    sp.wait_ge(store_s, 16 * NS)

            @block.gpsimd
            def _(pool):
                link = Chain(pool, parts_link_s)
                pool.memset(two, -1.0)
                pool.memset(sig, -1.0).then_inc(fill_s, 1)
                if x_in is not None:
                    pool.wait_ge(high_s, 1)
                    pool.tensor_tensor(m.w_gate[:, E:2 * E], raw_route, m.w_gate[:, 0:E].bitcast(F32),
                                       ALU.subtract).then_inc(low_s, 1)
                    for n in range(len(raws)):
                        raw, high, low = raw_and_parts(n)
                        pool.wait_ge(high_s, n + 2)
                        pool.tensor_tensor(low, raw, high.bitcast(F32), ALU.subtract).then_inc(low_s, 1)

                def weights(h):
                    w, p, rest = wts[:, halves[h]], parts[:, halves[h]], sig[:, halves[h], 0:E]

                    pool.wait_ge(chosen_s, h + 1)
                    link(pool.tensor_tensor(w, w, inv[:, halves[h]].unsqueeze(2).to_broadcast([P, NT // 2, E]),
                                            ALU.mult))
                    link(pool.tensor_copy(p[:, :, 0], w))
                    pool.tensor_tensor(p[:, :, 1], w, p[:, :, 0], ALU.subtract)
                    link(pool.tensor_tensor(rest, w, p[:, :, 0], ALU.subtract))
                    pool.tensor_tensor(p[:, :, 2], rest, p[:, :, 1], ALU.subtract).then_inc(parts_s, 1)

                def residual(s):
                    tiles = slice(s * TPS, (s + 1) * TPS)
                    pool.wait_ge(half_s, s + 1)
                    pool.tensor_tensor(m.x[:, tiles], x_n[:, tiles], m.x[:, tiles], ALU.add).then_inc(residual_s, 1)

                def slab(s):
                    first = isinstance(s, int)
                    for c in range(N):
                        n = s * N + c
                        rows = slice(0, P) if c < NCH else slice(0, I)
                        if not first:
                            pool.wait_ge(down_s, n - N + 1)
                        pool.wait_ge(hidh_s, n + 1)
                        pool.tensor_tensor(hid_parts[1][c][rows], hid[c % 3][rows],
                                           hid_parts[0][c][rows].bitcast(F32), ALU.subtract).then_inc(hidl_s, 1)
                        if first and c % 2 == 1:
                            residual(c // 2)

                weights(0)
                weights(1)
                slab(0)
                with pool.Fori(1, NS) as s:
                    slab(s)

            @block.scalar
            def _(act):
                if x_in is not None:
                    act.wait_ge(route_s, 32)
                    act.activation(m.w_gate[:, 0:E], raw_route, ACT.Copy).then_inc(high_s, 1)
                def high_parts(numbers):
                    for n in numbers if x_in is not None else []:
                        raw, high, _ = raw_and_parts(n)
                        act.wait_ge(weights_s[n], 32 if n == 2 else 16)
                        act.activation(high, raw, ACT.Copy).then_inc(high_s, 1)

                ln_scalar(act, lambda s: high_parts(([0], [1, 2], [3, 4], [])[s]))
                for h in range(2):
                    act.wait_ge(z_s, h + 1)
                    act.activation(wts[:, halves[h]], wts[:, halves[h]], ACT.Tanh, scale=0.5).then_inc(tanh_s, 1)

                def weights_out(h):
                    act.wait_ge(wt_psum_s, h + 1)
                    for k in range(2):
                        act.activation(wT[0:3 * E, (2 * h + k) * SLAB:(2 * h + k + 1) * SLAB],
                                       wT_ps[:, k * SLAB:(k + 1) * SLAB], ACT.Copy).then_inc(wt_s, 1)

                def tanh(s, c):
                    act.wait_ge(gate_s, s * N + c + 1)
                    rows = slice(0, P) if c < NCH else slice(0, I)
                    gate = gate_ps[c % 2] if c < NCH else shared_ps[rows]
                    act.activation(th[c % 3][rows], gate, ACT.Tanh, scale=0.5).then_inc(th_s, 1)

                def high(s, c, first):
                    n = s * N + c
                    rows = slice(0, P) if c < NCH else slice(0, I)
                    if not first:
                        act.wait_ge(down_s, n - N + 1)
                    act.wait_ge(hid_s, n + 1)
                    act.activation(hid_parts[0][c][rows], hid[c % 3][rows], ACT.Copy).then_inc(hidh_s, 1)

                def sum_out(s):
                    act.wait_ge(down_s, (s + 1) * N)
                    if not isinstance(s, int) or s > 0:
                        act.wait_ge(turned_s, s)
                    act.activation(out_sb, out_ps, ACT.Copy).then_inc(sum_s, 1)

                def slab(s, first, last):
                    for c in range(N):
                        if c + 1 < N:
                            tanh(s, c + 1)
                        elif not last:
                            tanh(s + 1, 0)
                        if c == DOWN_LAG and not first:
                            sum_out(s - 1)
                        if first and c == 0:
                            weights_out(1)
                        high(s, c, first)
                        if first and c % 2 == 1:
                            tiles = slice(c // 2 * TPS, (c // 2 + 1) * TPS)
                            act.activation(x_n[:, tiles], x_n[:, tiles], ACT.Copy, scale=0.5).then_inc(half_s, 1)

                tanh(0, 0)
                weights_out(0)
                slab(0, True, False)
                with act.Fori(1, NS - 1) as s:
                    slab(s, False, False)
                slab(NS - 1, False, True)
                sum_out(NS - 1)

            @block.vector
            def _(dve):
                link = Chain(dve, link_s)
                ln_vector(dve, link, x_in_s if x_in is not None else None)
                if x_in is not None:
                    dve.wait_ge(route_s, 32)
                route_link = Chain(dve, route_link_s)

                def logits(h):
                    w = wts[:, halves[h]]
                    dve.wait_ge(logits_s, h + 1)
                    route_link(dve.tensor_tensor(
                        w, logit_ps[h][:, :, 1], m.gate_b[:, :].unsqueeze(1).to_broadcast([P, NT // 2, E]),
                        ALU.add))
                    dve.tensor_tensor(w, w, logit_ps[h][:, :, 0], ALU.add).then_inc(z_s, 1)

                def route(h):
                    tiles = range(NT)[halves[h]]

                    dve.wait_ge(tanh_s, h + 1)
                    route_link(dve.tensor_scalar(sig[:, halves[h], 0:E], wts[:, halves[h]], 0.5, 0.5,
                                                 ALU.mult, ALU.add))
                    for n in tiles:
                        ins = dve.max(top[:, n], sig[:, n, 0:E])
                    route_link(ins)
                    route_link(dve.tensor_copy(two[:, halves[h], 0:2], top[:, halves[h], 0:2]))
                    for n in tiles:
                        ins = dve.match_replace(rep[:, n], two[:, n], sig[:, n], 0.0)
                    route_link(ins)
                    dve.tensor_tensor(wts[:, halves[h]], sig[:, halves[h], 0:E], rep[:, halves[h], 0:E],
                                      ALU.subtract)
                    route_link(dve.tensor_tensor(sums[:, halves[h]], top[:, halves[h], 0],
                                                 top[:, halves[h], 1], ALU.add))
                    dve.reciprocal(inv[:, halves[h]], sums[:, halves[h]]).then_inc(chosen_s, 1)

                dve.wait_ge(fill_s, 1)
                logits(0)
                ln_low(dve, NS - 1)
                route(0)
                logits(1)
                route(1)
                if x_in is not None:
                    dve.wait_ge(low_s, len(raws) + 1)
                base = link.done

                def chunk(s, c):
                    n = s * N + c
                    k = base + s * (2 * NCH + 1) + 2 * c
                    dve.wait_ge(th_s, n + 1)
                    shared = c == NCH
                    rows = slice(0, I) if shared else slice(0, P)
                    gate = shared_ps[rows] if shared else gate_ps[c % 2]
                    dve.scalar_tensor_tensor(silu[c % 3][rows], th[c % 3][rows], 1.0, gate,
                                             ALU.add, ALU.mult).then_inc(link_s, 1)
                    dve.wait_ge(link_s, k + 1)
                    if not isinstance(s, int) or n >= 3:
                        dve.wait_ge(hidl_s, n - 2)
                    if shared:
                        dve.scalar_tensor_tensor(hid[c % 3][rows], silu[c % 3][rows], 0.25, shared_ps[I:2 * I],
                                                 ALU.mult, ALU.mult).then_inc(hid_s, 1)
                        return
                    dve.wait_ge(up_s, s * NCH + c + 1)
                    dve.tensor_tensor(gated, silu[c % 3], up_ps[c % 2], ALU.mult).then_inc(link_s, 1)
                    dve.wait_ge(link_s, k + 2)
                    dve.wait_ge(w_s, s * NCH + c + 1)
                    dve.tensor_tensor(hid[c % 3], gated, wt_ps[c % 2], ALU.mult).then_inc(hid_s, 1)

                def update(s):
                    dve.wait_ge(residual_s, NS)
                    dve.wait_ge(turned_s, s + 1)
                    xs = m.x[:, bass.ts(s, TPS)]
                    dve.tensor_tensor(xs, shared_ps.rearrange("p (n c) -> p n c", n=TPS), xs,
                                      ALU.add).then_inc(x_s, 1)

                def slab(s):
                    for c in range(N):
                        chunk(s, c)
                        if c == TURN_AT + 2 and not isinstance(s, int):
                            update(s - 1)

                slab(0)
                with dve.Fori(1, NS) as s:
                    slab(s)
                if x_out is None:
                    statistics(dve, m, range((NS - 1) * TPS)).then_inc(stats_s, 1)
                    dve.wait_ge(stats_s, 1)
                    aggregate(dve, m, range((NS - 1) * TPS))
                update(NS - 1)

            @block.tensor
            def _(pe):
                if x_in is not None:
                    pe.wait_ge(const_s, 32)

                def logits(s):
                    if x_in is not None and s == 0:
                        pe.wait_ge(low_s, 1)
                    pe.wait_ge(xt_low, s + 1)
                    for n in range(s * TPS, (s + 1) * TPS):
                        to = logit_ps[n // (NT // 2)][:, n % (NT // 2)]
                        pe.matmul(to.rearrange("p k e -> p (k e)"), xT[0][:, n * P:(n + 1) * P],
                                  m.w_gate[:, :], start=True, stop=False, skip_group_check=True)
                        ins = pe.matmul(to[:, 0], xT[1][:, n * P:(n + 1) * P], m.w_gate[:, 0:E],
                                        start=False, stop=True, skip_group_check=True)
                    if s % 2 == 1:
                        ins.then_inc(logits_s, 1)

                ln_tensor(pe, logits)

                def turn_weights(h):
                    pe.wait_ge(parts_s, h + 1)
                    if h == 1:
                        pe.wait_ge(wt_s, 2)
                    for n, tile in enumerate(range(NT)[halves[h]]):
                        ins = pe.transpose(wT_ps[:, n * P:(n + 1) * P],
                                           parts[:, tile].rearrange("p k e -> p (k e)"), m.ident_bf[:, :])
                    ins.then_inc(wt_psum_s, 1)

                def product(out, n_weights, s):
                    for k, (a, b) in enumerate(PARTS2):
                        ins = pe.matmul(out, m.w_gu[a][:, n_weights * P:(n_weights + 1) * P],
                                        xT[b][:, bass.ts(s, SLAB)], start=(k == 0), stop=(k == 2))
                    return ins

                def products(s, c):
                    if c == NCH:
                        product(shared_ps, 2 * NCH, s).then_inc(gate_s, 1)
                        return
                    gate_up(s, c)
                    weights(s, c)

                def gate_up(s, c):
                    product(gate_ps[c % 2], c, s).then_inc(gate_s, 1)
                    product(up_ps[c % 2], NCH + c, s).then_inc(up_s, 1)

                def weights(s, c):
                    pe.matmul(wt_ps[c % 2], m.select[0:3 * E, c * P:(c + 1) * P],
                              wT[0:3 * E, bass.ts(s, SLAB)], start=True, stop=True).then_inc(w_s, 1)

                def down(s, c):
                    if x_in is not None and isinstance(s, int) and s == c == 0:
                        pe.wait_ge(low_s, len(raws) + 1)
                    pe.wait_ge(hidl_s, s * N + c + 1)
                    rows = slice(0, P) if c < NCH else slice(0, I)
                    for k, (a, b) in enumerate(PARTS2):
                        ins = pe.matmul(out_ps, m.w_dn[a][rows, c * C:(c + 1) * C], hid_parts[b][c][rows],
                                        start=(c == 0 and k == 0), stop=(c == NCH and k == 2),
                                        skip_group_check=True)
                    ins.then_inc(down_s, 1)

                def turn(s):
                    pe.wait_ge(sum_s, s + 1)
                    for j in range(TPS):
                        ins = pe.transpose(shared_ps[:, j * P:(j + 1) * P], out_sb[:, j * P:(j + 1) * P],
                                           m.ident[:, :])
                    ins.then_inc(turned_s, 1)

                def slab(s, first, last):
                    for c in range(N):
                        nxt = c + 2
                        if nxt <= NCH:
                            if nxt < NCH:
                                pe.wait_ge(hid_s, s * N + nxt - 1)
                            elif first:
                                pe.wait_ge(wt_s, NS)
                            else:
                                pe.wait_ge(x_s, s)
                            products(s, nxt)
                        elif not last:
                            pe.wait_ge(hid_s, s * N + NCH - 1 + nxt - N)
                            products(s + 1, nxt - N)
                        if c >= DOWN_LAG:
                            if c == DOWN_LAG and not first:
                                pe.wait_ge(sum_s, s)
                            down(s, c - DOWN_LAG)
                        elif not first:
                            down(s - 1, c - DOWN_LAG + N)
                        if c == TURN_AT and not first:
                            turn(s - 1)

                if x_in is not None:
                    pe.wait_ge(low_s, 3)
                    pe.wait_ge(select_s, 16)
                for c in range(2):
                    gate_up(0, c)
                turn_weights(0)
                pe.wait_ge(wt_s, 1)
                for c in range(2):
                    weights(0, c)
                turn_weights(1)
                slab(0, True, False)
                with pe.Fori(1, NS - 1) as s:
                    slab(s, False, False)
                slab(NS - 1, False, True)
                for c in range(N - DOWN_LAG, N):
                    down(NS - 1, c)
                turn(NS - 1)


STORE_INCS = (16 * 6, 16)
ROW_INCS = 16 * 2 * len(RUNS)


QK_ORDER = [(s, w) for b in range(B) for w in range(2) for s in (2 * b, 2 * b + 1)]
LATE = 5


def part_of(parts, s, w, k):
    b, at = s * SLAB // T, s * SLAB % T
    return parts[:, b, w, k, at:at + SLAB]


def late_rests(y_tiles):
    flat = y_tiles.rearrange("p n c -> p (n c)")
    return [flat[:, n * SLAB:(n + 1) * SLAB] for n in range(len(QK_ORDER) - LATE)]


def store_q(eng, scratch, parts, b, n, done, which=(0, 1, 2)):
    for k in which:
        to = scratch[b, 0, k].rearrange("c t -> (c t)").rearrange(
            "(e g n j t) -> n (e g) j t", e=DH, g=H // GH, n=2, j=GH)[n]
        eng.dma_start(to, parts[:, b, 0, k, n * SLAB:(n + 1) * SLAB]).then_inc(done, 16)


def store_k(eng, scratch, parts, b, done, which=slice(0, 3)):
    eng.dma_start(scratch[b, 1, which].rearrange("k c t -> c k t"), parts[:, b, 1, which]).then_inc(done, 16)


def load_rows(eng, m, scratch, b, g, groups, done, which=(0, 1), runs=RUNS):
    size = groups * GH * T
    at = g * GH * T
    for w in which:
        rows = (m.q, m.k)[w]
        parts = scratch[b, w].rearrange("k (e g) c -> k e (g c)", e=DH)[:, :, at:at + size]
        for lo, hi in runs:
            first, step = SPLIT[lo][w], SPLIT[lo + 1][w] - SPLIT[lo][w] if hi - lo > 1 else 1
            assert [x[w] for x in SPLIT[lo:hi]] == [first + step * n for n in range(hi - lo)]
            if step:
                source = parts[first:first + hi - lo]
            else:
                source = parts[first].unsqueeze(0).to_broadcast([hi - lo, DH, size])
            eng.dma_start(rows[lo * DH:hi * DH, at:at + size], source).then_inc(done, 16)


def qkv_phase(nc, m, d, scratch, parts, y_tiles):
    with ExitStack() as ctx:
        def sem(what):
            return ctx.enter_context(nc.semaphore(f"qkv_{what}"))

        def sb(what, cols, dt=F32):
            return ctx.enter_context(nc.sbuf_tensor(f"qkv_{what}_s", [P, cols], dt))[:, :]

        x_n = sb("x_n", NT * C).rearrange("p (n c) -> p n c", n=NT)
        xT = sb("xT", NT * P)
        w_qkv = m.vcur[:, 0:3 * C]
        b_v = m.vcur[:, 3 * C:4 * C]
        w_qk = m.vcur[:, 4 * C:6 * C]
        rest = [sb(f"rest{n}", SLAB) for n in range(LATE)] + late_rests(y_tiles)
        v = m.v[:, :].rearrange("p (b g t k) -> p b g t k", b=B, g=H // GH, t=TB)
        bank = [m.ps[:, b * 512:(b + 1) * 512] for b in range(8)]
        qk_ps = bank[4:8] + bank[0:4]
        v_ps = bank[4:8]

        link_s = sem("link")
        ln = [link_s, sem("var"), sem("sd"), sem("xn"), sem("xt_psum"), sem("xt"), None]
        xt_ready = ln[5]
        w_s, w_qk_s, qk_s, v_s = sem("weights"), sem("qk_columns"), sem("qk_psum"), sem("v_psum")
        zero_s = sem("zeros")
        p3_urgent_s = sem("part3_urgent")
        full_s = sem("full")
        p1_s, r1_s, p2_s, p3_s = sem("part1"), sem("rest1"), sem("part2"), sem("part3")
        vdone_s = sem("v_sbuf")
        ln_vector, _, ln_scalar, ln_tensor = layer_norm(m, x_n, xT, None, ln, (NS - 1) * TPS)
        w_incs = 16 * 3
        order = QK_ORDER

        urgent = 2 * NS // B - 1

        def part(s, w, k):
            return part_of(parts, s, w, k)

        with nc.Block() as block:

            @block.sync
            def _(sp):
                sp.dma_start(w_qkv, d["W_qkv"]).then_inc(w_s, 16)
                sp.dma_start(b_v, d["b_qkv"][2 * C:3 * C].partition_broadcast(P)).then_inc(w_s, 16)
                sp.dma_start(m.b_qk[:, :], d["b_qk"]).then_inc(w_s, 16)
                for h in range(2):
                    sp.dma_start(heads_of(m.decay[h]), d["decay"][:, 0:GH * P].rearrange("p (j t) -> p j t", j=GH)
                                 ).then_inc(m.decay_loaded[h], 16)
                q_stored, k_stored = m.stored[0]
                for k, ready in enumerate((p1_s, p2_s, p3_s)):
                    for n in range(2):
                        sp.wait_ge(ready, n + 1)
                        store_q(sp, scratch, parts, 0, n, q_stored[k], (k,))
                for k, ready in enumerate((p1_s, p2_s)):
                    sp.wait_ge(ready, urgent + 1)
                    store_k(sp, scratch, parts, 0, k_stored[k], slice(k, k + 1))
                    sp.wait_ge(q_stored[k], 2 * 16)
                    load_rows(sp, m, scratch, 0, 0, 1, m.rows_0, (0,), RUNS[k:k + 1])
                sp.wait_ge(p3_s, urgent)
                sp.wait_ge(p3_urgent_s, 1)
                store_k(sp, scratch, parts, 0, k_stored[2], slice(2, 3))
                sp.wait_ge(q_stored[2], 2 * 16)
                load_rows(sp, m, scratch, 0, 0, 1, m.rows_0, (0,), RUNS[2:])
                for k, run in enumerate(RUNS[::-1]):
                    sp.wait_ge(k_stored[k], 16)
                    load_rows(sp, m, scratch, 0, 0, 1, m.rows_0, (1,), (run,))

            @block.scalar
            def _(act):
                def first(n):
                    act.wait_ge(full_s, n + 1)
                    act.activation(part(*order[n], 0), rest[n], ACT.Copy).then_inc(p1_s, 1)

                def second(n):
                    act.wait_ge(r1_s, n + 1)
                    act.activation(part(*order[n], 1), rest[n], ACT.Copy).then_inc(p2_s, 1)

                def beside(s):
                    if s == 1:
                        first(0)
                        first(1)
                        second(0)

                ln_scalar(act, beside)
                for n in range(1, LATE):
                    if n == urgent:
                        second(n)
                    if n + 1 < len(order):
                        first(n + 1)
                    if n != urgent:
                        second(n)
                for n in range(LATE + 1, len(order)):
                    first(n)

            @block.gpsimd
            def _(pool):
                for table in m.decay:
                    pool.memset(table.rearrange("p (k t) -> p k t", t=P)[:, 0::2], 0.0).then_inc(zero_s, 1)
                pool.memset(m.max_parts[:, :], 0.0).then_inc(zero_s, 1)
                pool.wait_ge(zero_s, 3)
                pool.wait_ge(w_s, w_incs)
                pool.tensor_copy(w_qk.rearrange("p (w e h) -> p w h e", w=2, e=DH),
                                 w_qkv[:, 0:2 * C].rearrange("p (w h e) -> p w h e", w=2, e=DH)).then_inc(w_qk_s, 1)
                for n, (s, w) in enumerate(order[:LATE]):
                    if n == urgent:
                        continue
                    pool.wait_ge(p2_s, n + 1)
                    pool.tensor_tensor(part(s, w, 2), rest[n], part(s, w, 1), ALU.subtract).then_inc(p3_s, 1)

            @block.vector
            def _(dve):
                link = Chain(dve, link_s)
                ln_vector(dve, link)
                dve.wait_ge(w_s, w_incs)

                def full(n):
                    s, w = order[n]
                    dve.wait_ge(qk_s, n + 1)
                    dve.tensor_scalar(rest[n], qk_ps[n], m.b_qk[:, w:w + 1], SCALE if w == 0 else 1.0,
                                      ALU.add, ALU.mult).then_inc(full_s, 1)

                full(0)
                for n, (s, w) in enumerate(order[:LATE]):
                    if n != urgent:
                        full(n + 1)
                    dve.wait_ge(p1_s, n + 1)
                    dve.tensor_tensor(rest[n], rest[n], part(s, w, 0), ALU.subtract).then_inc(r1_s, 1)
                    if n == urgent:
                        full(n + 1)
                        dve.wait_ge(p2_s, n + 1)
                        dve.tensor_tensor(part(s, w, 2), rest[n], part(s, w, 1),
                                          ALU.subtract).then_inc(p3_urgent_s, 1)
                for n in range(LATE + 1, len(order)):
                    full(n)
                for s in range(NS):
                    b, t = divmod(s * TPS, TB)
                    dve.wait_ge(v_s, s + 1)
                    dve.tensor_tensor(
                        v[:, b, :, t:t + TPS], v_ps[s].rearrange("p (t g k) -> p g t k", t=TPS, g=H // GH),
                        b_v.rearrange("p (g k) -> p g k", g=H // GH).unsqueeze(2).to_broadcast(
                            [P, H // GH, TPS, GH * DH]), ALU.add).then_inc(vdone_s, 1)

            @block.tensor
            def _(pe):
                def products(numbers):
                    for n in numbers:
                        s, w = order[n]
                        if n == 0:
                            pe.wait_ge(w_s, w_incs)
                            pe.wait_ge(w_qk_s, 1)
                        pe.wait_ge(xt_ready, s + 1 if s < NS // 2 else NS)
                        pe.matmul(qk_ps[n], w_qk[:, w * C:(w + 1) * C], xT[:, s * SLAB:(s + 1) * SLAB],
                                  start=True, stop=True).then_inc(qk_s, 1)

                ln_tensor(pe, lambda s: products(([0, 1], [2], [3], [])[s]))
                products(range(2 * B, 4 * B))
                for n in range(NT):
                    if n % TPS == 0:
                        pe.wait_ge(full_s, n // TPS + 1)
                    ins = pe.matmul(v_ps[n // TPS][:, n % TPS * P:(n % TPS + 1) * P], xT[:, n * P:(n + 1) * P],
                                    w_qkv[:, 2 * C:3 * C], start=True, stop=True)
                    if n % TPS == TPS - 1:
                        ins.then_inc(v_s, 1)


QUADS = 2 * TB
UNITS = QUADS * GH
TILES = GH * TB
HALF = TILES // 2
AHEAD = TILES // 2 + 6
LAG = 2
SLOTS = 4
TURN = 3


def quad(q):
    n, s = divmod(q, TB)
    return (s + n * TB // 2) % TB, n


def has_diagonal(q):
    s, n = quad(q)
    return s // (TB // 2) == n


def tile_of(b):
    return (0, AHEAD + b) if b < TILES - AHEAD else (1, b - (TILES - AHEAD))


def tile_place(t):
    h, r = divmod(t, HALF)
    j, i = divmod(r, TB // 2)
    return h, j, h * (TB // 2) + i


LAST_TILE = (TILES - AHEAD - 1, TILES - AHEAD + HALF - 1)


def double_uses():
    uses = []
    for b in range(TILES):
        uses.append(("tile", b))
        for h in range(2):
            if b == LAST_TILE[1 - h] + 2:
                uses.append(("both", h))
    return uses


BODY_USES = double_uses()
BEFORE_USES = [x for x in BODY_USES if x == ("both", 0) or (x[0] == "tile" and x[1] >= TILES - AHEAD)]
LAST_USES = [x for x in BODY_USES if x not in BEFORE_USES] + [("result", 0), ("result", 1)]


def use(g, what):
    if isinstance(g, int) and g < 0:
        return BEFORE_USES.index(what)
    order = LAST_USES if isinstance(g, int) and g == NG - 1 else BODY_USES
    return g * len(BODY_USES) + len(BEFORE_USES) + order.index(what)


def turn_of(g, what):
    return use(g if isinstance(g, int) else 2, what) % 2


WIDE_FROM = (LAST_TILE[0] + 2) // 2 + 1


def bank_of(last, u):
    first = WIDE_FROM * GH
    if not last or u < first:
        return u % 2, 2
    return u % 4, 2 if u < first + 2 else 4


def key_order(i):
    half = TB // 2
    own = [i // half * half + r for r in range(half)]
    other = [s for s in range(TB) if s not in own]
    at = i % half
    if at < half // 2:
        return own + other, (0, at + 1), (1 - at, 2)
    return other + own, (half + at, TB), (1, 1 + half - at)


def attention_phase(nc, m, d, scratch, qk_parts, y_tiles):
    assert len(BODY_USES) % 2 == 0
    with ExitStack() as ctx:
        def sem(what):
            return ctx.enter_context(nc.semaphore(f"att_{what}"))

        def sb(what, cols, dt=F32):
            return ctx.enter_context(nc.sbuf_tensor(f"att_{what}_s", [P, cols], dt))[:, :]

        probs = sb("probs", SLOTS * GH * SLAB).rearrange("p (s j t) -> p s j t", s=SLOTS, j=GH)
        decay_exp = sb("decay_exp", GH * P)
        junk = sb("junk", 4 * P).rearrange("p (n t) -> p n t", n=2)
        v_group = m.vcur[:, :].rearrange("p (t j k) -> p t j k", t=TB, j=GH)
        double = [m.ps[:, 0:1024], m.ps[:, 1024:2048]]
        score_ps = [m.ps[:, 2048:2560], m.ps[:, 2560:3072]]
        spare = double[1 - turn_of(NG - 1, ("result", 0))]
        wide_ps = score_ps + [spare[:, 0:SLAB], spare[:, SLAB:2 * SLAB]]
        acc_ps = m.ps[:, 3072:4096]
        parts = m.max_parts[:, :].rearrange("p (k h n) -> p h k n", k=3, h=2)
        recip = m.recip[:, :].rearrange("p (h t j) -> p h t j", h=2, t=TB // 2)

        late1_s = sem("late_rest")
        late2_s = sem("late_part2")
        late3_s = sem("late_part3")
        vinit_s = sem("v_init")
        exp_table_s = sem("decay_exp")
        d_ready_s = sem("double_ready")
        d_free_s = sem("double_free")
        link_s = sem("link")
        recip_s = sem("recip")
        top_s = sem("maxima")
        parts_s = sem("max_parts")
        rows_s = sem("max_rows")
        score_s = sem("scores")
        exp_s = sem("exp")
        decay_s = sem("decayed")
        pv_s = sem("pv")
        y_s = sem("y")
        vg_s = sem("v_group")

        late = list(zip(range(LATE, len(QK_ORDER)), late_rests(y_tiles)))

        def late_part(n, k):
            return part_of(qk_parts, *QK_ORDER[n], k)

        def q_cols(base, half, j, start, size):
            return bass.ds(base + (half * GH + j) * SLAB + start, size)

        def k_cols(base, j, start, size):
            return bass.ds(base + j * T + start, size)

        def base_of(g):
            return (g & 3) * (GH * T)

        with nc.Block() as block:

            @block.sync
            def _(sp):
                def rows(g, h, body):
                    sp.wait_ge(d_free_s, use(body, ("both", h)) + 1)
                    for k in range(3):
                        sp.dma_start(m.q[ROWS_1 + k:ROWS_1 + k + 1, q_cols(base_of(g), h, 0, 0, GH * SLAB)].rearrange(
                            "o (n t) -> o n t", n=HALF), m.max_rows[k * TILES + h * HALF:k * TILES + (h + 1) * HALF, :]
                        ).then_inc(rows_s, 16)

                def table(h, g):
                    sp.dma_start(heads_of(m.decay[h]), table_of("decay", g).rearrange("p (j t) -> p j t", j=GH)
                                 ).then_inc(m.decay_loaded[h], 16)

                def table_of(name, g):
                    return d[name][:, bass.ds(g * (GH * P), GH * P)]

                sp.dma_start(decay_exp, table_of("decay_exp", 0)).then_inc(exp_table_s, 16)
                load_rows(sp, m, scratch, 0, 1, 1, m.rows)
                load_rows(sp, m, scratch, 0, 2, H // GH - 2, m.rows)
                sp.dma_start(m.w_proj[:, :], d["W_proj"]).then_inc(m.proj_loaded, 16)
                sp.dma_start(m.b_proj[:, :], d["b_proj"].partition_broadcast(P)).then_inc(m.proj_loaded, 16)
                for n in range(2):
                    before = NS + n + 1 - LATE
                    if before > 0:
                        sp.wait_ge(late3_s, before)
                    store_q(sp, scratch, qk_parts, 1, n, m.stored[1][0])
                sp.wait_ge(late3_s, len(late))
                store_k(sp, scratch, qk_parts, 1, m.stored[1][1])
                rows(0, 0, -1)
                table(0, 1)
                for g in range(NG):
                    if 1 <= g <= NG - H // GH:
                        if g == 1:
                            for w in range(2):
                                sp.wait_ge(m.stored[1][w], STORE_INCS[w])
                        sp.wait_ge(m.rows, ROW_INCS * (g + 1))
                        sp.wait_ge(score_s, g * UNITS)
                        load_rows(sp, m, scratch, 1, g - 1, 1, m.rows)
                    rows(g, 1, g)
                    if g == NG - 1:
                        break
                    table(1, g + 1)
                    sp.wait_ge(decay_s, (g + 1) * TB)
                    sp.dma_start(decay_exp, table_of("decay_exp", g + 1)).then_inc(exp_table_s, 16)
                    rows(g + 1, 0, g)
                    if g < NG - 2:
                        table(0, g + 2)

            @block.gpsimd
            def _(pool):
                pool.memset(m.vcur[:, :], 0.0).then_inc(vinit_s, 1)
                pool.wait_ge(vinit_s, 1)
                pool.memset(v_group[:, :, :, DH:DH + 1], 1.0).then_inc(vinit_s, 1)
                pool.wait_ge(vinit_s, 2)
                for n, rest in late:
                    pool.tensor_tensor(rest, rest, late_part(n, 0), ALU.subtract).then_inc(late1_s, 1)
                for k, (n, rest) in enumerate(late):
                    pool.wait_ge(late2_s, k + 1)
                    pool.tensor_tensor(late_part(n, 2), rest, late_part(n, 1), ALU.subtract).then_inc(late3_s, 1)

                def split(g, h):
                    top = m.max_a[:, h * HALF:(h + 1) * HALF]
                    rest = m.max_b[:, h * HALF:(h + 1) * HALF]
                    pool.wait_ge(top_s, 2 * g + h + 1)
                    pool.tensor_tensor(parts[:, h, 1], top, parts[:, h, 0], ALU.subtract)
                    pool.tensor_tensor(rest, top, parts[:, h, 0], ALU.subtract).then_inc(link_s, 1)
                    pool.wait_ge(link_s, 2 * g + h + 1)
                    pool.tensor_tensor(parts[:, h, 2], rest, parts[:, h, 1], ALU.subtract).then_inc(parts_s, 1)

                def body(g, first, last):
                    pool.wait_ge(exp_table_s, 16 * (g + 1))
                    for q in range(QUADS):
                        if q == (LAST_TILE[0] + 1) // 2:
                            split(g, 1)
                        if q == (LAST_TILE[1] + 1) // 2 and not last:
                            split(g + 1, 0)
                        if q == 1:
                            if not first:
                                pool.wait_ge(pv_s, g * QUADS)
                            pool.tensor_copy(v_group[:, :, :, 0:DH], m.v[:, bass.ts(g, TB * GH * DH)].rearrange(
                                "p (t j k) -> p t j k", t=TB, j=GH)).then_inc(vg_s, 1)
                        if not has_diagonal(q):
                            continue
                        pool.wait_ge(exp_s, g * UNITS + (q + 1) * GH)
                        at = quad(q)[0] % (TB // 2) * P
                        block_ = probs[:, q % SLOTS, :, at:at + P]
                        pool.tensor_tensor(block_, block_, decay_exp.rearrange("p (j t) -> p j t", j=GH),
                                           ALU.mult).then_inc(decay_s, 1)

                split(0, 0)
                body(0, True, False)
                with pool.Fori(1, NG - 1) as g:
                    body(g, False, False)
                body(NG - 1, False, True)

            @block.scalar
            def _(act):
                def result(g, h):
                    act.wait_ge(pv_s, g * QUADS + (h + 1) * TB)
                    act.activation(m.y[:, h * SLAB:(h + 1) * SLAB], acc_ps[:, h * SLAB:(h + 1) * SLAB],
                                   ACT.Copy).then_inc(y_s, 1)

                def body(g, first, last):
                    for q in range(QUADS):
                        if not first or q >= SLOTS:
                            act.wait_ge(pv_s, g * QUADS + q - SLOTS + 1)
                        for j in range(GH):
                            u = q * GH + j
                            act.wait_ge(score_s, g * UNITS + u + 1)
                            act.activation(probs[:, q % SLOTS, j], wide_ps[bank_of(last, u)[0]],
                                           ACT.Exp).then_inc(exp_s, 1)
                        if q == LAG - 1 and not first:
                            result(g - 1, 1)
                        if q == TB + LAG - 1:
                            result(g, 0)

                for k, (n, rest) in enumerate(late):
                    act.wait_ge(late1_s, k + 1)
                    act.activation(late_part(n, 1), rest, ACT.Copy).then_inc(late2_s, 1)
                body(0, True, False)
                with act.Fori(1, NG - 1) as g:
                    body(g, False, False)
                body(NG - 1, False, True)
                result(NG - 1, 1)

            @block.vector
            def _(dve):
                def tile(g, b):
                    ahead, t = tile_of(b)
                    h, j, i = tile_place(t)
                    u = use(g, ("tile", b))
                    dve.wait_ge(d_ready_s, u + 1)
                    turn = turn_of(g, ("tile", b))
                    ps = double[turn]
                    if t % HALF == 0:
                        dve.wait_ge(m.decay_loaded[h], 16 * (g + ahead + 1))
                    if not isinstance(u, int) or u > 1:
                        dve.wait_ge(d_free_s, u - 1)
                    _, (lo, hi), (from_, to) = key_order(i)
                    table = m.decay[h][:, (2 * j + from_) * P:(2 * j + to) * P]
                    dve.tensor_reduce(m.max_a[:, t:t + 1], ps[:, hi * P:T] if lo == 0 else ps[:, 0:lo * P],
                                      AX_X, ALU.max)
                    dve.tensor_tensor_reduce(
                        junk[:, turn, 0:(hi - lo) * P], ps[:, lo * P:hi * P], table, 1.0, -3.0e38, ALU.add, ALU.max,
                        m.max_b[:, t:t + 1]).then_inc(d_free_s, 1)

                def top(g, h, body):
                    dve.wait_ge(d_free_s, use(body, ("tile", LAST_TILE[1 - h])) + 1)
                    half = slice(h * HALF, (h + 1) * HALF)
                    dve.tensor_tensor(parts[:, h, 0], m.max_a[:, half], m.max_b[:, half], ALU.max)
                    dve.tensor_tensor(m.max_a[:, half], m.max_a[:, half], m.max_b[:, half], ALU.max).then_inc(top_s, 1)

                def maxima(g, h, ps):
                    if not (isinstance(g, int) and g == 0 and h == 0):
                        dve.wait_ge(rows_s, 48 * (2 * g + h))
                    return dve.tensor_copy(m.max_rows[0:3 * TILES, :],
                                           ps[0:3 * TILES, SLAB:SLAB + P // 2].bitcast(BF16))

                def result(g, h, ps):
                    ps = ps[:, 0:SLAB].rearrange("p (t j k) -> p t j k", t=TB // 2, j=GH)
                    dve.reciprocal(recip[:, h], ps[:, :, :, DH]).then_inc(recip_s, 1)
                    dve.wait_ge(recip_s, 2 * g + h + 1)
                    to = y_tiles[:, h * TB // 2:(h + 1) * TB // 2, bass.ts(g, GH * DH)].rearrange(
                        "p t (j k) -> p t j k", j=GH)
                    return dve.tensor_tensor(
                        to, ps[:, :, :, 0:DH], recip[:, h].unsqueeze(3).to_broadcast([P, TB // 2, GH, DH]), ALU.mult)

                def body(g, uses, first):
                    for kind, which in uses:
                        if kind == "tile":
                            tile(g, which)
                            if which in LAST_TILE:
                                h = 1 - LAST_TILE.index(which)
                                top(g + 1 - h, h, g)
                            continue
                        u = use(g, (kind, which))
                        dve.wait_ge(d_ready_s, u + 1)
                        dve.wait_ge(d_free_s, u)
                        ps = double[turn_of(g, (kind, which))]
                        if kind == "both":
                            ins = maxima(g + 1 - which, which, ps)
                        if not first or (g == 0 and which == 0):
                            ins = result(g - (which if kind == "both" else 0), which, ps)
                        ins.then_inc(d_free_s, 1)

                body(-1, BEFORE_USES, True)
                body(0, BODY_USES, True)
                with dve.Fori(1, NG - 1) as g:
                    body(g, BODY_USES, False)
                body(NG - 1, LAST_USES[:-2], False)
                dve.wait_ge(m.proj_loaded, 32)
                dve.tensor_tensor(m.x, m.x, m.b_proj[:, :].unsqueeze(1).to_broadcast([P, NT, C]), ALU.add)
                body(NG - 1, LAST_USES[-2:], False)

            @block.tensor
            def _(pe):
                def double_free(g, what):
                    u = use(g, what)
                    if not isinstance(u, int) or u > 1:
                        pe.wait_ge(d_free_s, u - 1)

                def tile(g, b, bank, base):
                    ahead, t = tile_of(b)
                    h, j, i = tile_place(t)
                    if bank == 0:
                        double_free(g, ("tile", b))
                    order = key_order(i)[0]
                    half = TB // 2
                    ins = pe.matmul(double[turn_of(g, ("tile", b))][:, bank * SLAB:(bank + 1) * SLAB],
                                    m.q[0:ROWS_1, q_cols(base[ahead], h, j, i % half * P, P)],
                                    m.k[0:ROWS_1, k_cols(base[ahead], j, order[bank * half] * P, SLAB)],
                                    start=True, stop=True)
                    if bank == 1:
                        ins.then_inc(d_ready_s, 1)

                def both(body, h, with_result):
                    double_free(body, ("both", h))
                    if with_result:
                        result(body - h, h, body, ("both", h))
                    pe.wait_ge(parts_s, 2 * (body + 1 - h) + h + 1)
                    pe.transpose(double[turn_of(body, ("both", h))][0:3 * TILES, SLAB:SLAB + P // 2].bitcast(BF16),
                                 m.max_parts[:, :], m.ident_bf[:, :]).then_inc(d_ready_s, 1)

                def result(g, h, body, what):
                    pe.wait_ge(y_s, 2 * g + h + 1)
                    for t in range(TB // 2):
                        ins = pe.transpose(double[turn_of(body, what)][:, t * P:(t + 1) * P],
                                           m.y[:, h * SLAB + t * P:h * SLAB + (t + 1) * P], m.ident[:, :])
                    return ins

                def result_alone(h):
                    what = ("result", h)
                    double_free(NG - 1, what)
                    result(NG - 1, h, NG - 1, what).then_inc(d_ready_s, 1)

                def scores(g, q, j, base):
                    u = q * GH + j
                    s, n = quad(q)
                    bank, back = bank_of(isinstance(g, int) and g == NG - 1, u)
                    if back == 4 and u == WIDE_FROM * GH + 2:
                        pe.wait_ge(d_free_s, use(g, ("both", 1)) + 1)
                    elif not isinstance(g, int) or g > 0 or u >= 2:
                        pe.wait_ge(exp_s, g * UNITS + u - back + 1)
                    pe.matmul(wide_ps[bank], m.k[0:ROWS_2, k_cols(base, j, s * P, P)],
                              m.q[0:ROWS_2, q_cols(base, n, j, 0, SLAB)],
                              start=True, stop=True).then_inc(score_s, 1)

                def pv(g, q):
                    s, n = quad(q)
                    if has_diagonal(q):
                        pe.wait_ge(decay_s, g * TB + sum(has_diagonal(x) for x in range(q + 1)))
                    else:
                        pe.wait_ge(exp_s, g * UNITS + (q + 1) * GH)
                    if q == 0:
                        pe.wait_ge(vg_s, g + 1)
                    if q % TB == 0 and (not isinstance(g, int) or g > 0):
                        pe.wait_ge(y_s, 2 * g - 1 + n)
                    for j in range(GH):
                        ins = pe.matmul(acc_ps[32 * j:32 * (j + 1), n * SLAB:(n + 1) * SLAB], v_group[:, s, j],
                                        probs[:, q % SLOTS, j], start=(q % TB == 0), stop=(q % TB == TB - 1),
                                        skip_group_check=True)
                    ins.then_inc(pv_s, 1)

                base_regs = [pe.alloc_register(f"base_{k}") for k in range(2)]

                def body(g, uses, first):
                    for q in range(QUADS):
                        if q % 4 == 0:
                            base = [base_of(g + ahead) for ahead in range(2)]
                            if not isinstance(g, int):
                                for k, x in enumerate(base):
                                    pe.reg_mov(base_regs[k], x)
                                base = [pe.snap(x, min_val=0, max_val=(H // GH - 1) * GH * T) for x in base_regs]
                        if q % TB == 0:
                            pe.wait_ge(rows_s, 48 * (2 * g + q // TB + 1))
                        if q == (TILES - AHEAD) // 2 and ("both", 0) in uses:
                            pe.wait_ge(m.rows, ROW_INCS * (2 if first else g))
                        if q == TB + TURN and ("result", 0) in uses:
                            result_alone(0)
                        two = [("tile", b) in uses for b in (2 * q, 2 * q + 1)]
                        scores(g, q, 0, base[0])
                        if two[0]:
                            tile(g, 2 * q, 0, base)
                        scores(g, q, 1, base[0])
                        if two[0]:
                            tile(g, 2 * q, 1, base)
                        if two[1]:
                            tile(g, 2 * q + 1, 0, base)
                        scores(g, q, 2, base[0])
                        if two[1]:
                            tile(g, 2 * q + 1, 1, base)
                        scores(g, q, 3, base[0])
                        if q >= LAG:
                            pv(g, q - LAG)
                        elif not first:
                            pv(g - 1, QUADS - LAG + q)
                        for h in range(2):
                            if ("both", h) in uses and LAST_TILE[1 - h] + 2 == 2 * q + 1:
                                both(g, h, not first or h == 0)

                pe.wait_ge(m.bias_loaded, 16 * 2)
                pe.wait_ge(m.rows_0, ROW_INCS)
                for kind, which in BEFORE_USES:
                    if kind == "tile":
                        for bank in range(2):
                            tile(-1, which, bank, (None, base_of(0)))
                    else:
                        both(-1, which, False)
                body(0, BODY_USES, True)
                with pe.Fori(1, NG - 1) as g:
                    body(g, BODY_USES, False)
                body(NG - 1, LAST_USES, False)
                for q in range(QUADS - LAG, QUADS):
                    pv(NG - 1, q)
                result_alone(1)


def project_phase(nc, m, y):
    with ExitStack() as ctx:
        def sem(what):
            return ctx.enter_context(nc.semaphore(f"proj_{what}"))

        yT = ctx.enter_context(nc.sbuf_tensor("yT_s", [P, NT * P], F32))[:, :]
        turned_s, yt_s, out_s, x_s, stats_s = sem("turned"), sem("yT"), sem("out"), sem("x"), sem("stats")
        link_s, var_s, sd_s = sem("link"), sem("var"), sem("sd")
        variance, root, inverse = inverse_deviation(m, range((NS - 1) * TPS))

        with nc.Block() as block:

            @block.scalar
            def _(act):
                for s in range(NS):
                    act.wait_ge(turned_s, s + 1)
                    act.activation(yT[:, s * SLAB:(s + 1) * SLAB], m.ps[:, s * 512:(s + 1) * 512],
                                   ACT.Copy).then_inc(yt_s, 1)
                act.wait_ge(var_s, 1)
                root(act).then_inc(sd_s, 1)

            @block.vector
            def _(dve):
                for s in range(NS):
                    dve.wait_ge(out_s, s + 1)
                    xs = m.x[:, s * TPS:(s + 1) * TPS]
                    dve.tensor_tensor(xs, m.ps[:, (4 + s) * 512:(5 + s) * 512].rearrange("p (n c) -> p n c", n=TPS),
                                      xs, ALU.add).then_inc(x_s, 1)
                    if s > 0:
                        dve.wait_ge(x_s, s)
                        statistics(dve, m, range((s - 1) * TPS, s * TPS)).then_inc(stats_s, 1)
                dve.wait_ge(stats_s, NS - 1)
                link = Chain(dve, link_s)

                def beside(k):
                    n = (NS - 1) * TPS + k
                    statistics(dve, m, range(n, n + 1))

                dve.wait_ge(x_s, NS)
                link(aggregate(dve, m, range((NS - 1) * TPS)), lambda: beside(0))
                variance(dve).then_inc(var_s, 1)
                beside(1)
                dve.wait_ge(sd_s, 1)
                inverse(dve, link, lambda k: beside(2 + k))

            @block.tensor
            def _(pe):
                def products(s):
                    pe.wait_ge(yt_s, s + 1)
                    for n in range(s * TPS, (s + 1) * TPS):
                        ins = pe.matmul(m.ps[:, 2048 + n * P:2048 + (n + 1) * P], yT[:, n * P:(n + 1) * P],
                                        m.w_proj[:, :], start=True, stop=True)
                    ins.then_inc(out_s, 1)

                for s in range(NS):
                    for n in range(s * TPS, (s + 1) * TPS):
                        b, t = divmod(n, TB)
                        ins = pe.transpose(m.ps[:, n * P:(n + 1) * P], y[:, t, b * P:(b + 1) * P], m.ident[:, :])
                    ins.then_inc(turned_s, 1)
                    if s > 0:
                        products(s - 1)
                products(NS - 1)


def build(nc, d, x_in, out, scratch):
    with ExitStack() as ctx:
        m = allocate(nc, ctx)
        ffn_phase(nc, m, "ffn1", d, x_in, None, 0)
        with (nc.sbuf_tensor("qk_parts", [P, B * 2 * 3 * T], BF16) as parts,
              nc.sbuf_tensor("decay", [P, 2 * TABLE], F32) as decay,
              nc.sbuf_tensor("y_tiles", [P, NT * P], F32) as y):
            m.decay = [decay[:, h * TABLE:(h + 1) * TABLE] for h in range(2)]
            y = y[:, :].rearrange("p (t c) -> p t c", t=TB)
            parts = parts[:, :].rearrange("p (b w k t) -> p b w k t", b=B, w=2, k=3)
            qkv_phase(nc, m, d, scratch, parts, y)
            attention_phase(nc, m, d, scratch, parts, y)
            project_phase(nc, m, y)
        ffn_phase(nc, m, "ffn2", d, None, out, NT)


_INS = ["L0_attn_x", "L0_attn_W_qkv", "L0_attn_b_qkv", "L0_attn_W_proj", "L0_attn_b_proj", "L0_ffn_gate_w",
        "L0_ffn_gate_b", "L0_ffn_shared_wg", "L0_ffn_shared_wu", "L0_ffn_shared_wd", "L0_ffn_experts_wg",
        "L0_ffn_experts_wu", "L0_ffn_experts_wd"]


def kernel(**inputs):
    import concourse.bacc as bacc
    from concourse.bass_utils import run_bass_kernel_spmd

    nc = bacc.Bacc("TRN2", target_bir_lowering=False, num_devices=1)
    arrays, d = {}, {}
    given = {k: np.ascontiguousarray(inputs[k]) for k in _INS}
    given["L0_attn_b_qk"] = np.ascontiguousarray(
        given["L0_attn_b_qkv"][:2 * C].reshape(2, H, DH).transpose(2, 1, 0).reshape(C, 2))
    for name, a in {**given, **constants()}.items():
        key = f"in_{name}_dram"
        arrays[key] = a
        short = name.replace("L0_ffn_", "").replace("L0_attn_", "")
        d[short] = nc.dram_tensor(key, a.shape, mybir.dt.from_np(a.dtype), kind="ExternalInput").ap()
    out = nc.dram_tensor("out_0_dram", (B, T, C), F32, kind="ExternalOutput").ap()
    tiled = "b (t p) c -> p (b t) c"
    scratch = nc.dram_tensor("parts_dram", (B, 2, 3, C, T), BF16, kind="Internal").ap()
    build(nc, d, d["x"].rearrange(tiled, p=P), out.rearrange(tiled, p=P), scratch)
    r = run_bass_kernel_spmd(nc, [arrays], core_ids=[0])
    return r.results[0]["out_0_dram"]
```
